# Optimizing a Trainium2 kernel written in Bass

```python
import numpy as np
import jax
import jax.numpy as jnp

def _softmax(x, axis=-1):
    return jax.nn.softmax(x, axis=axis)

def _gelu(x):
    return jax.nn.gelu(x, approximate=True)

def _silu(x):
    return jax.nn.silu(x)

def _sigmoid(x):
    return jax.nn.sigmoid(x)

def _layernorm(x, axis=-1, eps=1e-05):
    m = jnp.mean(x, axis=axis, keepdims=True)
    v = jnp.var(x, axis=axis, keepdims=True)
    return (x - m) / jnp.sqrt(v + eps)

def _scatter_add(tgt, idx, src, axis=0):
    return tgt.at[idx].add(src)

def _segment_sum(src, seg, n):
    return jax.ops.segment_sum(src, seg, n)
kernel_name = 'mk_xattn_ffn_d1_seqx_r2_feb909'

def setup_inputs(seed: int=0):
    np.random.seed(seed)
    _w = jnp.asarray

    def _rec_inputs():
        import jax
        import jax.numpy as jnp
        _rk = jax.random.key(seed)
        x = 0.0002417 + 0.9998 * jax.random.normal(jax.random.fold_in(_rk, 1), (8, 512, 512), jnp.float32)
        _lenS = 512 - jax.random.randint(jax.random.fold_in(_rk, 7), (8,), 0, max(1, 512 // 4) + 1, jnp.int32)
        _lenS2 = 120 - jax.random.randint(jax.random.fold_in(_rk, 8), (8,), 0, max(1, 120 // 4) + 1, jnp.int32)
        _ctx_1024P = jax.random.normal(jax.random.fold_in(_rk, 11), (8, 16, 512), jnp.float32)
        _ctx_1024c = jax.random.dirichlet(jax.random.fold_in(_rk, 511), 0.3 * jnp.ones((16,), jnp.float32), (8, 120))
        _ctx_1024t = jnp.einsum('bsk,bkd->bsd', _ctx_1024c, _ctx_1024P)
        _ctx_1024t = _ctx_1024t * jax.lax.rsqrt(jnp.mean(jnp.square(_ctx_1024t)) + 1e-12) * 0.953939
        ctx_1024 = 7.22013e-05 + 1.00017 * (_ctx_1024t + 0.3 * jax.random.normal(jax.random.fold_in(_rk, 611), (8, 120, 512), jnp.float32))
        return (x, ctx_1024)
    x, ctx_1024 = _rec_inputs()

    def _L0_xattn_setup():
        import jax, jax.numpy as jnp
        import numpy as np
        D_MODEL = 512
        B, S = (4, 1024)
        key = jax.random.key(seed)
        ks = jax.random.split(key, 10)
        s = 1.0 / np.sqrt(D_MODEL)
        return {'k': jax.random.normal(ks[0], (B, S, D_MODEL), jnp.float32), 'v': jax.random.normal(ks[1], (B, S, D_MODEL), jnp.float32), 'q': jax.random.normal(ks[2], (B, S, D_MODEL), jnp.float32), 'Wk': jax.random.normal(ks[3], (D_MODEL, D_MODEL), jnp.float32) * s, 'Wv': jax.random.normal(ks[4], (D_MODEL, D_MODEL), jnp.float32) * s, 'bv': jnp.zeros((D_MODEL,), jnp.float32), 'Wq': jax.random.normal(ks[5], (D_MODEL, D_MODEL), jnp.float32) * s, 'bq': jnp.zeros((D_MODEL,), jnp.float32), 'Wo': jax.random.normal(ks[6], (D_MODEL, D_MODEL), jnp.float32) * s, 'bo': jnp.zeros((D_MODEL,), jnp.float32)}
    _L0_xattn_all = _L0_xattn_setup()
    _L0_xattn_in = {k: v for k, v in _L0_xattn_all.items() if k in ('Wk', 'Wv', 'bv', 'Wq', 'bq', 'Wo', 'bo')}
    del _L0_xattn_all

    def _L0_ffn_setup():
        import jax, jax.numpy as jnp
        import numpy as np
        H = 512
        I = 512
        E = 8
        key = jax.random.key(seed)
        ks = jax.random.split(key, 8)
        s = 0.02
        x = jax.random.normal(ks[0], (4, 1024, H), dtype=jnp.float32)
        Wg = jax.random.normal(ks[1], (H, E), dtype=jnp.float32) * s
        bg = jnp.zeros((E,), dtype=jnp.float32)
        W1 = jax.random.normal(ks[2], (E, H, I), dtype=jnp.float32) * s
        b1 = jnp.zeros((E, I), dtype=jnp.float32)
        W2 = jax.random.normal(ks[3], (E, I, H), dtype=jnp.float32) * s
        b2 = jnp.zeros((E, H), dtype=jnp.float32)
        return {'x': x, 'Wg': Wg, 'bg': bg, 'W1': W1, 'b1': b1, 'W2': W2, 'b2': b2}
    _L0_ffn_all = _L0_ffn_setup()
    _L0_ffn_in = {k: v for k, v in _L0_ffn_all.items() if k in ('Wg', 'bg', 'W1', 'b1', 'W2', 'b2')}
    del _L0_ffn_all
    return {'x': x, 'ctx_1024': ctx_1024, 'L0_xattn_Wk': _L0_xattn_in['Wk'], 'L0_xattn_Wv': _L0_xattn_in['Wv'], 'L0_xattn_bv': _L0_xattn_in['bv'], 'L0_xattn_Wq': _L0_xattn_in['Wq'], 'L0_xattn_bq': _L0_xattn_in['bq'], 'L0_xattn_Wo': _L0_xattn_in['Wo'], 'L0_xattn_bo': _L0_xattn_in['bo'], 'L0_ffn_Wg': _L0_ffn_in['Wg'], 'L0_ffn_bg': _L0_ffn_in['bg'], 'L0_ffn_W1': _L0_ffn_in['W1'], 'L0_ffn_b1': _L0_ffn_in['b1'], 'L0_ffn_W2': _L0_ffn_in['W2'], 'L0_ffn_b2': _L0_ffn_in['b2']}

def reference(x, ctx_1024, L0_xattn_Wk, L0_xattn_Wv, L0_xattn_bv, L0_xattn_Wq, L0_xattn_bq, L0_xattn_Wo, L0_xattn_bo, L0_ffn_Wg, L0_ffn_bg, L0_ffn_W1, L0_ffn_b1, L0_ffn_W2, L0_ffn_b2):
    import jax
    import jax.numpy as jnp

    def _L0_xattn_ref(k, v, q, Wk, Wv, bv, Wq, bq, Wo, bo):
        import jax, jax.numpy as jnp
        import numpy as np
        D_MODEL = 512
        B, S = (4, 1024)
        kp = jnp.einsum('bsd,ed->bse', k, Wk)
        vp = jnp.einsum('bsd,ed->bse', v, Wv) + bv
        qp = jnp.einsum('bsd,ed->bse', q, Wq) + bq
        scale = 1.0 / jnp.sqrt(jnp.float32(kp.shape[-1]))
        scores = jnp.einsum('bqd,bkd->bqk', qp, kp) * scale
        probs = jax.nn.softmax(scores, axis=-1)
        ctx = jnp.einsum('bqk,bkd->bqd', probs, vp)
        return jnp.einsum('bqd,ed->bqe', ctx, Wo) + bo

    def _L0_ffn_ref(x, Wg, bg, W1, b1, W2, b2):
        import jax, jax.numpy as jnp
        import numpy as np
        H = 512
        I = 512
        E = 8
        B, S, Hd = x.shape
        xf = x.reshape(-1, Hd)
        logits = xf @ Wg + bg
        gates = jax.nn.softmax(logits, axis=-1)
        idx = jnp.argmax(gates, axis=-1)
        h = jax.nn.gelu(jnp.einsum('th,ehi->tei', xf, W1) + b1, approximate=False)
        y = jnp.einsum('tei,eih->teh', h, W2) + b2
        out = jnp.take_along_axis(y, idx[:, None, None], axis=1)[:, 0, :]
        return out.reshape(B, S, Hd)
    x = x + _L0_xattn_ref(ctx_1024, ctx_1024, _layernorm(x, axis=-1), L0_xattn_Wk, L0_xattn_Wv, L0_xattn_bv, L0_xattn_Wq, L0_xattn_bq, L0_xattn_Wo, L0_xattn_bo)
    x = x + _L0_ffn_ref(_layernorm(x, axis=-1), L0_ffn_Wg, L0_ffn_bg, L0_ffn_W1, L0_ffn_b1, L0_ffn_W2, L0_ffn_b2)
    return x

_drawn_inputs = setup_inputs


def setup_inputs(seed=0):
    import zlib

    import numpy as np

    out = dict(_drawn_inputs(seed))
    spreads = {'L0_xattn_bv': (0.0, 0.1),
     'L0_xattn_bq': (0.0, 0.1),
     'L0_xattn_bo': (0.0, 0.1),
     'L0_ffn_bg': (0.0, 0.1),
     'L0_ffn_b1': (0.0, 0.351),
     'L0_ffn_b2': (0.0, 0.1)}
    factors = {}
    for name, (base, spread) in spreads.items():
        noise = np.random.default_rng([zlib.crc32(name.encode()), seed]).standard_normal(out[name].shape)
        drawn = base * np.exp(spread * noise) if base else spread * noise
        out[name] = jnp.asarray(drawn.astype(out[name].dtype))
    for name, factor in factors.items():
        out[name] = (out[name] * factor).astype(out[name].dtype)
    return out
```

```python
import concourse.bass as bass
from concourse import mybir
from contextlib import ExitStack

F32 = mybir.dt.float32
F16 = mybir.dt.float16
I32 = mybir.dt.int32
ALU = mybir.AluOpType
ACT = mybir.ActivationFunctionType
AX = mybir.AxisListType

P = 128
D = 512
C = D // P
B = 8
S = 512
K = 120
E = 8
T = B * S
EPS = 1e-5
SCALE = float(D) ** -0.5
NT = T // P
U = 8
G = 4
NTURN = NT // U
ROW = D + 4
SPAN = P + T
DUMMY = E * SPAN
NJ = (T + E * (P - 1)) // P
R = 3
NJTURN = NJ // R
OOB = T + 1


def need(eng, sem, value):
    if not (isinstance(value, int) and value <= 0):
        eng.wait_ge(sem, value)


def wait_apart(eng, sem, value, waits):
    if isinstance(value, int):
        return need(eng, sem, value)
    eng.wait_ge(sem, value)
    eng.sem_inc(waits, 1)


class Count:

    def __init__(self, sem, base=0):
        self.sem, self.base, self.n = sem, base, 0

    def inc(self, ins):
        self.n += 1
        return ins.then_inc(self.sem, 1)

    @property
    def value(self):
        return self.base + self.n


def is_tile(t):
    return not isinstance(t, int) or 0 <= t < NT


def build(nc, x, ctx_in, Wk, Wv, bv, Wq, bq, Wo, bo, Wg, bg, W1, b1, W2, b2, out):
    x_rows = x.rearrange("b s d -> (b s) d")
    out_rows = out.rearrange("b s d -> (b s) d")
    routed = nc.dram_tensor("routed_rows", (E * SPAN + P, ROW), F32, kind="Internal").ap()

    ctx = ExitStack()
    with ctx:
        def sb(name, shape, dt=F32):
            return ctx.enter_context(nc.sbuf_tensor(name, shape, dt))

        def sem(name):
            return ctx.enter_context(nc.semaphore(name))

        wall = sb("expert_weights", [P, E * 2 * C * D])
        w_of = wall[:, :].rearrange("p (e m n) -> p e m n", e=E, m=2)
        keys = sb("keys_then_b1", [P, B * C * P])
        vals = sb("values_then_b2", [P, B * D])
        work = sb("work", [P, U * ROW + 4 * D])
        key_bias = sb("key_bias", [1, B * P])
        val_gate = sb("value_gate_columns", [K, B * E])
        ident = sb("identity", [P, P])
        ones_f = sb("ones_f32", [P, P])
        ones_h = sb("ones_f16", [P, P], F16)
        before = sb("strictly_before", [P, P], F16)
        wg_sb = sb("gate_weights", [P, C, E])
        bg_bc = sb("gate_bias", [P, E])
        wg_mid = sb("gate_weights_centred", [P, C, E])
        vg_bias = sb("value_gate_bias", [P, E])
        base_row = sb("expert_base_rows", [P, E])
        first_pick = sb("first_pick_rank", [P, E])
        half = sb("minus_half", [P, NT])
        brow12 = sb("bias_rows", [3 * C, P])
        bcol = sb("bias_columns", [P, 3 * C])
        ucol = sb("key_bias_weights", [P, C])
        wo_gate = sb("wo_gate", [P, C, E])
        wv_gate = sb("wv_gate", [P, C, E])
        stats = sb("stats", [P, U, 6])
        mv1 = sb("mean_var_x", [P, NT, 2])
        mv2 = sb("mean_var_x1", [P, U, 2])
        ve1 = sb("var_eps_x", [P, NT])
        ve2 = sb("var_eps_x1", [P, U])
        rstd1 = sb("rstd_x", [P, NT])
        std1 = sb("std_x", [P, NT])
        negm1 = sb("neg_mean_x", [P, NT])
        nmr1 = sb("neg_mean_rstd_x", [P, NT])
        negmax = sb("neg_row_max", [P, U])
        rowsum = sb("row_sums", [P, U])
        rinv = sb("row_sum_inverses", [P, U])
        za = sb("gate_from_x", [P, U, E])
        z = sb("gate_logits", [P, U, E])
        zs = sb("gate_logits_scaled", [P, G, E])
        zl = sb("gate_logits_biased", [P, G, E])
        zt = sb("gate_scratch", [P, G, E])
        zm = sb("gate_max", [P, G])
        pick = sb("expert_one_hot", [P, G, E], F16)
        picks = sb("group_picks", [P, E], F16)
        seen = sb("picks_seen", [P, 2, E], F16)
        slot_i = sb("slot_index", [P, U], I32)
        cnt = sb("expert_counts", [P, E])
        ti = sb("tiles_int", [P, E], I32)
        cum = sb("tiles_cumulated", [P, 4, E])
        vrow = sb("last_tile_rows", [P, E])
        jota = sb("tile_numbers", [P, NJ])
        eota = sb("expert_numbers", [P, E])
        ge = sb("tile_expert_table", [P, NJ, E])
        tv = sb("tile_vectors", [P, 4, NJ])
        table = sb("tile_table", [P, 3, NJ], I32)

        rows = work[:, 0:U * ROW].rearrange("p (u r) -> p u r", u=U)
        rest = U * ROW
        xn = [work[:, rest + D * n:rest + D * (n + 1)] for n in range(2)]
        xnT = work[:, rest + 2 * D:rest + 3 * D].rearrange("p (c t) -> p c t", c=C)
        prob = [work[:, rest + 3 * D + P * n:rest + 3 * D + P * n + K] for n in range(2)]
        probT = [work[0:K, rest + 3 * D + 2 * P + P * n:rest + 3 * D + 2 * P + P * (n + 1)] for n in range(2)]
        ctx_nat = work[:, 0:B * D].rearrange("p (b n) -> p b n", b=B)
        kq = work[:, rest:rest + 4 * D].rearrange("p (c n) -> p c n", c=C)
        xs = w_of[:, E - 1, :, :].rearrange("p m n -> p (m n)").rearrange("p (u n) -> p u n", u=U)
        wk_sb, wq_sb = (w_of[:, 7, m, :].rearrange("p (c n) -> p c n", c=C) for m in range(2))
        wv_sb, wo_sb = (w_of[:, 6, m, :].rearrange("p (c n) -> p c n", c=C) for m in range(2))
        ov, woT = (w_of[:, 5, m, :].rearrange("p (c n) -> p c n", c=C) for m in range(2))
        ctxT = wall[:, 4 * 2 * C * D:4 * 2 * C * D + C * B * K].rearrange("p (c s) -> p c s", c=C)
        bv_bc = w_of[:, 3, 0, 0:D].rearrange("p (c t) -> p c t", c=C)
        bo_cb = w_of[:, 3, 0, D:2 * D].rearrange("p (c t) -> p c t", c=C)
        bo_bc = w_of[:, 3, 0, 2 * D:3 * D]
        val_bias = w_of[:, 3, 0, 3 * D:4 * D]
        pad_row = w_of[:, 3, 1, 0:ROW]
        at = [0]

        def carve(n):
            at[0] += n
            return work[:, at[0] - n:at[0]]

        rrow = [carve(ROW) for _ in range(R)]
        res = [carve(D) for _ in range(R)]
        xn2, x2T, hid, gel, gelT = (carve(D) for _ in range(5))
        assert at[0] <= U * ROW + 4 * D
        x2T = x2T.rearrange("p (c t) -> p c t", c=C)
        gelT = gelT.rearrange("p (c t) -> p c t", c=C)
        out_id = sb("output_ids", [P, R], I32)

        bank = [ctx.enter_context(nc.psum_tensor(f"bank{n}", [P, D], F32)) for n in range(8)]

        ld = {n: sem(f"loaded_{n}") for n in ("wk", "wq", "ctx", "wv", "wo", "wg", "bias", "bo", "bg")}
        w_in = sem("experts_loaded")
        b_in = sem("expert_biases_loaded")
        pad_out = sem("pad_rows_written")
        consts = sem("constants_ready")
        pool_seq = sem("pool_sequence")
        dve_seq = sem("vector_sequence")
        pool_waits = sem("pool_waits_passed")
        dve_waits = sem("vector_waits_passed")
        pre_mm = sem("preparation_products")
        pre_act = sem("preparation_copies_act")
        pre_dve = sem("preparation_copies_dve")
        xg_in = [sem(f"x_group_loaded_{g}") for g in range(2)]
        x_in = [sem(f"x_loaded_{u}") for u in range(U)]
        stats1 = sem("stats_of_x")
        scal1 = sem("scales_of_x")
        xn_ready = sem("xn_ready")
        tx_done = sem("xn_transposed")
        xT_done = sem("xnT_copied")
        s_done = sem("scores_done")
        s_read = sem("scores_read")
        exp_done = sem("exp_done")
        pt_done = sem("probs_transposed")
        pT_done = sem("probsT_copied")
        pv_done = sem("values_mixed")
        x1_done = sem("x1_done")
        stats2 = sem("stats_of_x1")
        scal2 = sem("logits_ready")
        picked = sem("experts_picked")
        ranked = sem("ranks_done")
        slotted = sem("slots_ready")
        sent = [sem(f"rows_routed_{g}") for g in range(2)]
        pairs_counted = sem("picks_all_seen")
        counted = sem("experts_counted")
        tabled = sem("tile_table_ready")
        row_in = [sem(f"row_tile_loaded_{r}") for r in range(R)]
        xn2_ready = sem("xn2_ready")
        res_ready = sem("residual_ready")
        tx2_done = sem("xn2_transposed")
        x2T_done = sem("xn2T_copied")
        h_done = sem("hidden_done")
        hb_done = sem("hidden_biased")
        g_done = sem("gelu_done")
        tg_done = sem("gelu_transposed")
        gT_done = sem("geluT_copied")
        y_done = sem("expert_product_done")
        out_done = sem("output_tile_ready")
        out_sent = [sem(f"output_sent_{r}") for r in range(R)]

        NCONST = 11

        jobs = (["dve"] + ["dve"] + ["act"] * (C + 1 + B + C + C + 2 + 2 * C + 2) + ["dve"] * (2 + 2 * B))
        J_BIAS = 0
        J_GSUM = 1
        J_KQ = 2
        J_U = J_KQ + C
        J_CTX = J_U + 1
        J_WOT = J_CTX + B
        J_OV = J_WOT + C
        J_WOG = J_OV + C
        J_WVG = J_WOG + 1
        J_KEYS = J_WVG + 1
        J_KB = J_KEYS + 2 * C
        J_VB = J_KB + 2
        J_VGB = J_VB + 1
        J_VAL = J_VGB + 1
        NJOBS = J_VAL + 2 * B
        assert NJOBS == len(jobs)

        def copied(eng, n):
            same = sum(1 for who in jobs[:n + 1] if who == jobs[n])
            eng.wait_ge(pre_act if jobs[n] == "act" else pre_dve, same)

        block = ctx.enter_context(nc.Block())

        @block.sync
        def _(sp):
            def chunked(w):
                return w.rearrange("(c p) n -> p c n", p=P)

            def load_expert(e):
                sp.dma_start(w_of[:, e, 0, :].rearrange("p (c n) -> p c n", c=C), chunked(W1[e])).then_inc(w_in, 16)
                sp.dma_start(w_of[:, e, 1, :].rearrange("p (c n) -> p c n", c=C), chunked(W2[e])).then_inc(w_in, 16)

            sp.dma_start(wk_sb, chunked(Wk)).then_inc(ld["wk"], 16)
            sp.dma_start(wq_sb, chunked(Wq)).then_inc(ld["wq"], 16)
            sp.dma_start(ctx_nat[0:K, :, :], ctx_in.rearrange("b k d -> k b d")).then_inc(ld["ctx"], 16)
            sp.dma_start(wo_sb, chunked(Wo)).then_inc(ld["wo"], 16)
            sp.dma_start(wv_sb, chunked(Wv)).then_inc(ld["wv"], 16)
            sp.wait_ge(pre_mm, J_U + 1)
            for n in range(NT // G):
                need(sp, stats1, G * (n - 1))
                sp.dma_start(xs[:, G * (n % 2):G * (n % 2 + 1), :],
                             x_rows[P * G * n:P * G * (n + 1), :].rearrange("(t p) d -> p t d", p=P)).then_inc(xg_in[n % 2], 16)
                if n % 2 == 1 and n < 6:
                    load_expert(n // 2)
            sp.wait_ge(pre_mm, J_WVG + 1)
            load_expert(6)

            def load_x(t, u):
                need(sp, x1_done, 2 * t - 2 * U + 2)
                sp.dma_start(xs[:, u, :], x_rows[bass.ds(t * P, P), :]).then_inc(x_in[u], 16)

            for u in range(U):
                if u % G == 0:
                    sp.wait_ge(stats1, NT - G + u)
                load_x(u, u)
            sp.wait_ge(pre_mm, NJOBS)
            sp.wait_ge(pre_dve, sum(1 for who in jobs if who == "dve"))
            sp.wait_ge(pad_out, 16 * (E + 1))
            for e in (3, 4, 5):
                load_expert(e)
            with sp.Fori(1, NTURN) as i:
                for u in range(U):
                    load_x(i * U + u, u)
            sp.wait_ge(x1_done, 2 * NT)
            load_expert(E - 1)
            sp.wait_ge(pv_done, NT)
            sp.dma_start(keys[:, :], b1.rearrange("e d -> (e d)").partition_broadcast(P)).then_inc(b_in, 16)
            sp.dma_start(vals[:, :], b2.rearrange("e d -> (e d)").partition_broadcast(P)).then_inc(b_in, 16)
            for g in range(2):
                sp.wait_ge(sent[g], 16 * G * NTURN)
            sp.wait_ge(pad_out, 16 * (E + 1))
            sp.wait_ge(tabled, 1)
            with sp.Fori(0, NJTURN) as i:
                for r in range(R):
                    j = i * R + r
                    sp.wait_ge(res_ready, j + 1)
                    start = sp.value_load(table[0:1, 0, bass.ds(j, 1)], min_val=0, max_val=DUMMY)
                    sp.dma_start(rrow[r], routed[bass.ds(start, P), :]).then_inc(row_in[r], 16)

        @block.gpsimd
        def _(pool):
            seq = Count(pool_seq)

            def link(ins):
                seq.inc(ins)
                pool.wait_ge(pool_seq, seq.value)

            pool.sem_inc(res_ready, R)
            nc.gpsimd.memset(ones_f[:, :], 1.0).then_inc(consts, 1)
            nc.gpsimd.memset(ones_h[:, :], 1.0).then_inc(consts, 1)
            nc.gpsimd.memset(half[:, :], -0.5).then_inc(consts, 1)
            nc.gpsimd.memset(key_bias[:, :], 0.0).then_inc(consts, 1)
            nc.gpsimd.iota(seen[:, 0, :], pattern=[[SPAN // P, E]], base=1, channel_multiplier=0,
                           allow_small_or_imprecise_dtypes=True).then_inc(consts, 1)
            link(nc.gpsimd.memset(ident[:, :], 0.0))
            nc.gpsimd.affine_select(out=ident[:, :], in_=ident[:, :], compare_op=ALU.not_equal, fill=1.0, base=0,
                                    pattern=[[-1, P]], channel_multiplier=1).then_inc(consts, 1)
            link(nc.gpsimd.memset(before[:, :], 1.0))
            nc.gpsimd.affine_select(out=before[:, :], in_=before[:, :], compare_op=ALU.is_gt, fill=0.0, base=0,
                                    pattern=[[1, P]], channel_multiplier=-1).then_inc(consts, 1)
            nc.gpsimd.iota(base_row[:, :], pattern=[[SPAN, E]], base=P, channel_multiplier=0,
                           allow_small_or_imprecise_dtypes=True).then_inc(consts, 1)
            nc.gpsimd.iota(first_pick[:, :], pattern=[[-1, E]], base=E, channel_multiplier=0,
                           allow_small_or_imprecise_dtypes=True).then_inc(consts, 1)
            nc.gpsimd.iota(jota[:, :], pattern=[[1, NJ]], base=0, channel_multiplier=0,
                           allow_small_or_imprecise_dtypes=True).then_inc(consts, 1)
            nc.gpsimd.iota(eota[:, :], pattern=[[1, E]], base=0, channel_multiplier=0,
                           allow_small_or_imprecise_dtypes=True).then_inc(consts, 1)
            link(nc.gpsimd.memset(pad_row, 0.0))
            link(nc.gpsimd.memset(pad_row[:, D + 2:D + 3].bitcast(I32), OOB))
            ids = rows[:, :, D + 2].bitcast(I32)
            pool.wait_ge(pre_mm, J_CTX + B)
            for e in range(E + 1):
                pool.dma_start(routed[SPAN * e:SPAN * e + P, :], pad_row).then_inc(pad_out, 16)
            link(nc.gpsimd.iota(ids, pattern=[[P, U]], base=0, channel_multiplier=1))
            link(nc.gpsimd.memset(rows[:, :, D + 3], 0.0))
            pool.wait_ge(stats1, NT)
            link(nc.gpsimd.tensor_scalar(ve1[:, :], mv1[:, :, 1], EPS, 1.0, ALU.add, ALU.mult))
            link(nc.gpsimd.tensor_tensor(rstd1[:, :], ve1[:, :], half[:, :], ALU.pow))
            link(nc.gpsimd.tensor_scalar(negm1[:, :], mv1[:, :, 0], -1.0, 0.0, ALU.mult, ALU.add))
            nc.gpsimd.tensor_tensor(nmr1[:, :], negm1[:, :], rstd1[:, :], ALU.mult).then_inc(scal1, 1)
            nc.gpsimd.tensor_tensor(std1[:, :], ve1[:, :], rstd1[:, :], ALU.mult).then_inc(scal1, 1)

            def scale(c, n, g):
                gs = slice(G * g, G * (g + 1))
                wait_apart(pool, stats2, n + 1, pool_waits)
                c.inc(nc.gpsimd.tensor_scalar(ve2[:, gs], mv2[:, gs, 1], EPS, 1.0, ALU.add, ALU.mult))
                wait_apart(pool, pool_seq, c.value, pool_waits)
                c.inc(nc.gpsimd.tensor_tensor(rows[:, gs, D + 1], ve2[:, gs], half[:, 0:G], ALU.pow))
                wait_apart(pool, pool_seq, c.value, pool_waits)
                c.inc(nc.gpsimd.tensor_tensor(zs[:, :, :], z[:, gs, :],
                                              rows[:, gs, D + 1].unsqueeze(2).to_broadcast([P, G, E]), ALU.mult))
                wait_apart(pool, pool_seq, c.value, pool_waits)
                nc.gpsimd.tensor_tensor(zl[:, :, :], zs[:, :, :], bg_bc[:, :].unsqueeze(1).to_broadcast([P, G, E]),
                                        ALU.add).then_inc(scal2, 1)
                c.inc(nc.gpsimd.tensor_scalar(rows[:, gs, D], mv2[:, gs, 0], -1.0, 0.0, ALU.mult, ALU.add))
                wait_apart(pool, pool_seq, c.value, pool_waits)

            def route(n, g):
                wait_apart(pool, slotted, n + 1, pool_waits)
                for j in range(G * g, G * (g + 1)):
                    pool.indirect_dma_start(routed, bass.IndirectOffsetOnAxis(ap=slot_i[:, j:j + 1], axis=0),
                                            rows[:, j, :], None).then_inc(sent[g], 16)

            def renumber(c, i, g):
                gs = slice(G * g, G * (g + 1))
                wait_apart(pool, sent[g], i * 16 * G + 16 * G, pool_waits)
                c.inc(nc.gpsimd.tensor_scalar(ids[:, gs], ids[:, gs], float(P * U), 1.0, ALU.add, ALU.mult))
                wait_apart(pool, pool_seq, c.value, pool_waits)

            pool.wait_ge(ld["bg"], 16)
            per_turn = 2 * 5
            start = seq.value
            with pool.Fori(0, NTURN) as i:
                c = Count(pool_seq, start + i * per_turn)
                for g in range(2):
                    scale(c, 2 * i + g, g)
                    route(2 * i + g, g)
                    renumber(c, i, g)
                assert c.n == per_turn

            pool.wait_ge(b_in, 32)

            def normalise(j, r, turn):
                wait_apart(pool, row_in[r], 16 * turn + 16, pool_waits)
                wait_apart(pool, tx2_done, j, pool_waits)
                nc.gpsimd.tensor_scalar(xn2, rrow[r][:, 0:D], rrow[r][:, D:D + 1], rrow[r][:, D + 1:D + 2],
                                        ALU.add, ALU.mult).then_inc(xn2_ready, 1)
                wait_apart(pool, out_sent[r], 16 * turn, pool_waits)
                ex = pool.value_load(table[0:1, 2, bass.ds(j, 1)], min_val=0, max_val=(E - 1) * D)
                nc.gpsimd.tensor_copy(out_id[:, r:r + 1], rrow[r][:, D + 2:D + 3].bitcast(I32))
                nc.gpsimd.tensor_tensor(res[r], rrow[r][:, 0:D], vals[:, bass.ds(ex, D)],
                                        ALU.add).then_inc(res_ready, 1)

            def send(j, r):
                wait_apart(pool, out_done, j + 1, pool_waits)
                pool.indirect_dma_start(out_rows, bass.IndirectOffsetOnAxis(ap=out_id[:, r:r + 1], axis=0),
                                        res[r], None, bounds_check=T - 1, oob_is_err=False).then_inc(out_sent[r], 16)

            for j in range(R):
                normalise(j, j, 0)
                if j >= 2:
                    send(j - 2, j - 2)
            with pool.Fori(1, NJTURN) as i:
                for r in range(R):
                    j = i * R + r
                    normalise(j, r, i)
                    send(j - 2, (r - 2) % R)
            for j in (NJ - 2, NJ - 1):
                send(j, j % R)
            for r in range(R):
                pool.wait_ge(out_sent[r], 16 * NJTURN)

        @block.scalar
        def _(act):
            chunk_rows = "(c p) -> c p"
            act.dma_start(brow12[0:C, :], bq.rearrange(chunk_rows, p=P)).then_inc(ld["bias"], 16)
            act.dma_start(brow12[C:2 * C, :], bv.rearrange(chunk_rows, p=P)).then_inc(ld["bias"], 16)
            act.dma_start(brow12[2 * C:3 * C, :], bo.rearrange(chunk_rows, p=P)).then_inc(ld["bias"], 16)
            act.dma_start(wg_sb[:, :, :], Wg.rearrange("(c p) e -> p c e", p=P)).then_inc(ld["wg"], 16)
            act.dma_start(bo_bc, bo.partition_broadcast(P)).then_inc(ld["bo"], 16)
            act.dma_start(bg_bc[:, :], bg.partition_broadcast(P)).then_inc(ld["bg"], 16)

            def copy(n, dst, src, scale=1.0):
                assert jobs[n] == "act"
                act.wait_ge(pre_mm, n + 1)
                nc.scalar.activation(dst, src, ACT.Copy, scale=scale).then_inc(pre_act, 1)

            for k in range(C):
                n = J_KQ + k
                copy(n, kq[:, k, :], bank[n % 8][:, :], SCALE)
            n = J_U
            copy(n, ucol[:, :], bank[n % 8][:, 0:C], SCALE)
            for b in range(B):
                n = J_CTX + b
                copy(n, ctxT[:, :, K * b:K * (b + 1)], bank[n % 8][:, 0:C * K].rearrange("p (c s) -> p c s", c=C))
            for k in range(C):
                n = J_WOT + k
                copy(n, woT[:, k, :], bank[n % 8][:, :])
            for k in range(C):
                n = J_OV + k
                copy(n, ov[:, k, :], bank[n % 8][:, :])
            for n, dst in ((J_WOG, wo_gate), (J_WVG, wv_gate)):
                copy(n, dst[:, :, :], bank[n % 8][:, 0:C * E].rearrange("p (c e) -> p c e", c=C))
            for m in range(2 * C):
                n = J_KEYS + m
                c, h = m // 2, m % 2
                dst = keys[:, :].rearrange("p (b c k) -> p b c k", b=B, c=C)[:, 4 * h:4 * h + 4, c, 0:K]
                copy(n, dst, bank[n % 8][:, 0:4 * K].rearrange("p (b k) -> p b k", b=4))
            act.wait_ge(consts, NCONST)
            for h in range(2):
                n = J_KB + h
                copy(n, key_bias[:, :].rearrange("o (b k) -> o b k", b=B)[:, 4 * h:4 * h + 4, 0:K],
                     bank[n % 8][0:1, 0:4 * K].rearrange("p (b k) -> p b k", b=4))

            def normalise(t, j, turn):
                act.wait_ge(x_in[j], turn * 16 + 16)
                need(act, tx_done, t - 1)
                nc.scalar.activation(xn[j % 2], xs[:, j, :], ACT.Identity, bias=nmr1[:, bass.ds(t, 1)],
                                     scale=rstd1[:, bass.ds(t, 1)]).then_inc(xn_ready, 1)

            def xT(t, j):
                act.wait_ge(tx_done, t + 1)
                need(act, s_done, t)
                nc.scalar.activation(xnT, bank[0][:, :].rearrange("p (c t) -> p c t", c=C),
                                     ACT.Copy).then_inc(xT_done, 1)

            def exp(t, j):
                act.wait_ge(s_read, 2 * t + 2)
                need(act, pt_done, t - 1)
                nc.scalar.activation(prob[j % 2], bank[2 + j % 2][:, 0:K], ACT.Exp, bias=negmax[:, j:j + 1],
                                     accum_out=rowsum[:, j:j + 1]).then_inc(exp_done, 1)

            def pT(t, j):
                act.wait_ge(pt_done, t + 1)
                need(act, pv_done, t - 1)
                nc.scalar.activation(probT[j % 2], bank[4 + j % 2][0:K, 0:P], ACT.Copy).then_inc(pT_done, 1)

            def step(k, j, turn):
                if is_tile(k + 1):
                    normalise(k + 1, (j + 1) % U, turn + (j + 1) // U)
                if is_tile(k):
                    xT(k, j)
                if is_tile(k - 1):
                    exp(k - 1, (j - 1) % U)
                if is_tile(k - 2):
                    pT(k - 2, (j - 2) % U)

            act.wait_ge(scal1, 2)
            act.wait_ge(pre_mm, NJOBS)
            for k in range(-1, U - 1):
                step(k, k % U, k // U)
            with act.Fori(1, NTURN) as i:
                for j in range(U):
                    step(i * U + j - 1, (j - 1) % U, i + (j - 1) // U)
            for k in range(NT - 1, NT + 3):
                step(k, k % U, k // U)

            act.wait_ge(tabled, 1)
            act.wait_ge(sent[1], 16 * G * NTURN)

            def x2T_copy(j):
                act.wait_ge(tx2_done, j + 1)
                act.wait_ge(h_done, j)
                nc.scalar.activation(x2T, bank[0][:, :].rearrange("p (c t) -> p c t", c=C),
                                     ACT.Copy).then_inc(x2T_done, 1)

            def gelu(j):
                act.wait_ge(hb_done, j + 1)
                act.wait_ge(tg_done, j)
                nc.scalar.activation(gel, hid, ACT.Gelu).then_inc(g_done, 1)

            def gT_copy(j):
                act.wait_ge(tg_done, j + 1)
                act.wait_ge(y_done, j)
                nc.scalar.activation(gelT, bank[2][:, :].rearrange("p (c t) -> p c t", c=C),
                                     ACT.Copy).then_inc(gT_done, 1)

            x2T_copy(0)
            gelu(0)
            x2T_copy(1)
            gT_copy(0)
            with act.Fori(1, NJ - 1) as j:
                gelu(j)
                x2T_copy(j + 1)
                gT_copy(j)
            gelu(NJ - 1)
            gT_copy(NJ - 1)

        @block.vector
        def _(dve):
            seq = Count(dve_seq)

            def link(ins):
                seq.inc(ins)
                dve.wait_ge(dve_seq, seq.value)


            def ready(n):
                assert jobs[n] == "dve"
                dve.wait_ge(pre_mm, n + 1)

            n = J_BIAS
            ready(n)
            nc.vector.tensor_copy(bcol[:, :], bank[n % 8][:, 0:3 * C]).then_inc(pre_dve, 1)
            dve.wait_ge(pre_dve, 1)
            link(nc.vector.tensor_copy(bv_bc, bcol[:, C:2 * C].unsqueeze(2).to_broadcast([P, C, P])))
            link(nc.vector.tensor_copy(bo_cb, bcol[:, 2 * C:3 * C].unsqueeze(2).to_broadcast([P, C, P])))
            n = J_GSUM
            ready(n)
            dve.wait_ge(ld["wg"], 16)
            nc.vector.scalar_tensor_tensor(wg_mid[:, :, :], bank[n % 8][:, 0:C * E].rearrange("p (c e) -> p c e", c=C),
                                           -1.0 / D, wg_sb[:, :, :], ALU.mult, ALU.add).then_inc(pre_dve, 1)
            for n in range(NT // G):
                dve.wait_ge(xg_in[n % 2], 16 * (n // 2 + 1))
                for u in range(G):
                    seq.inc(nc.vector.bn_stats(stats[:, u, :], xs[:, G * (n % 2) + u, :]))
                dve.wait_ge(dve_seq, seq.value)
                for u in range(G):
                    nc.vector.bn_aggr(mv1[:, G * n + u, :], stats[:, u, :]).then_inc(stats1, 1)
                dve.wait_ge(stats1, G * (n + 1))
            dve.wait_ge(pre_dve, 2)
            keys4 = keys[:, :].rearrange("p (b c k) -> p b c k", b=B, c=C)
            for c in range(C):
                link(nc.vector.tensor_copy(keys4[:, :, c, K:P], wg_mid[:, c:c + 1, :].to_broadcast([P, B, E])))
            n = J_VB
            ready(n)
            dve.wait_ge(ld["bo"], 16)
            nc.vector.tensor_tensor(val_bias, bank[n % 8][:, :], bo_bc, ALU.add).then_inc(pre_dve, 1)
            n = J_VGB
            ready(n)
            nc.vector.tensor_copy(vg_bias[:, :], bank[n % 8][:, 0:E]).then_inc(pre_dve, 1)
            dve.wait_ge(pre_dve, 4)
            for b in range(B):
                n = J_VAL + 2 * b
                ready(n)
                nc.vector.tensor_tensor(vals[0:K, D * b:D * (b + 1)], bank[n % 8][0:K, :], val_bias[0:K, :],
                                        ALU.add).then_inc(pre_dve, 1)
                n += 1
                ready(n)
                nc.vector.tensor_tensor(val_gate[:, E * b:E * (b + 1)], bank[n % 8][0:K, 0:E], vg_bias[0:K, :],
                                        ALU.add).then_inc(pre_dve, 1)

            dve.wait_ge(ld["bg"], 16)
            dve.wait_ge(scal1, 2)

            def done(c):
                wait_apart(dve, dve_seq, c.value, dve_waits)

            def pick_experts(c, n, g):
                def link(ins):
                    c.inc(ins)
                    dve.wait_ge(dve_seq, c.value)

                def over_e(a):
                    return a.unsqueeze(2).to_broadcast([P, G, E])

                def over_t(a):
                    return a.unsqueeze(1).to_broadcast([P, G, E])

                dve.wait_ge(scal2, n + 1)
                link(nc.vector.tensor_reduce(zm[:, :], zl[:, :, :], AX.X, ALU.max))
                link(nc.vector.tensor_tensor(zt[:, :, :], zl[:, :, :], over_e(zm[:, :]), ALU.is_equal))
                link(nc.vector.tensor_tensor(zt[:, :, :], zt[:, :, :], over_t(first_pick[:, :]), ALU.mult))
                link(nc.vector.tensor_reduce(zm[:, :], zt[:, :, :], AX.X, ALU.max))
                nc.vector.tensor_tensor(pick[:, :, :], over_t(first_pick[:, :]), over_e(zm[:, :]),
                                        ALU.is_equal).then_inc(picked, 1)

            def place(c, n, g):
                gs = slice(G * g, G * (g + 1))

                def link(ins):
                    c.inc(ins)
                    dve.wait_ge(dve_seq, c.value)

                dve.wait_ge(ranked, n + 1)
                link(nc.vector.tensor_tensor(zt[:, :, :], bank[1][:, 0:G * E].rearrange("p (t e) -> p t e", t=G),
                                             pick[:, :, :], ALU.mult))
                with nc.allow_low_precision(reason="row numbers and counts below 64 are exact"):
                    nc.vector.tensor_reduce(slot_i[:, gs], zt[:, :, :], AX.X, ALU.add).then_inc(slotted, 1)
                    link(nc.vector.tensor_reduce(picks[:, :], pick[:, :, :].rearrange("p t e -> p e t"), AX.X,
                                                 ALU.add))
                link(nc.vector.tensor_tensor(seen[:, 1 - g, :], seen[:, g, :], picks[:, :], ALU.add))

            def read_scores(t, j):
                dve.wait_ge(s_done, t + 1)
                nc.vector.tensor_scalar(za[:, j, :], bank[2 + j % 2][:, K:P], std1[:, bass.ds(t, 1)], None,
                                        ALU.mult).then_inc(s_read, 1)
                nc.vector.tensor_reduce(negmax[:, j:j + 1], bank[2 + j % 2][:, 0:K], AX.X, ALU.max,
                                        negate=True).then_inc(s_read, 1)

            def mixed(c, t, j, turn):
                dve.wait_ge(exp_done, t + 1)
                c.inc(nc.vector.reciprocal(rinv[:, j:j + 1], rowsum[:, j:j + 1]))
                dve.wait_ge(dve_seq, c.value)
                dve.wait_ge(pv_done, t + 1)
                nc.vector.scalar_tensor_tensor(z[:, j, :], bank[4 + j % 2][:, P:P + E], rinv[:, j:j + 1],
                                               za[:, j, :], ALU.mult, ALU.add).then_inc(x1_done, 1)
                need(dve, sent[j // G], 16 * G * turn)
                nc.vector.scalar_tensor_tensor(rows[:, j, 0:D], bank[6 + j % 2][:, :], rinv[:, j:j + 1],
                                               xs[:, j, :], ALU.mult, ALU.add).then_inc(x1_done, 1)
                dve.wait_ge(x1_done, 2 * t + 2)
                c.inc(nc.vector.bn_stats(stats[:, j, :], rows[:, j, 0:D]))
                done(c)
                ins = nc.vector.bn_aggr(mv2[:, j, :], stats[:, j, :])
                if j % G == G - 1:
                    ins.then_inc(stats2, 1)
                else:
                    c.inc(ins)

            def step(c, k, j, turn):
                if j % G == 1 and is_tile(k - 9):
                    place(c, 2 * turn + (j - 9) // G, (j - 9) // G % 2)
                if is_tile(k - 1):
                    read_scores(k - 1, (j - 1) % U)
                if is_tile(k - 3):
                    mixed(c, k - 3, (j - 3) % U, turn if j >= 3 else turn - 1)
                if j % G == G - 1 and is_tile(k - 7):
                    pick_experts(c, 2 * turn + (j - 7) // G, (j - 7) // G % 2)

            for k in range(U):
                step(seq, k, k, 0)
            per_turn = U + 2 * U - 2 + 2 * (4 + 3)
            start = seq.value
            with dve.Fori(1, NTURN) as i:
                c = Count(dve_seq, start + i * per_turn - per_turn)
                for j in range(U):
                    step(c, i * U + j, j, i)
                assert c.n == per_turn, c.n
            c = Count(dve_seq, start + (NTURN - 1) * per_turn)
            for k in range(NT, NT + U):
                step(c, k, k % U, k // U)

            def link(ins):
                c.inc(ins)
                dve.wait_ge(dve_seq, c.value)

            nc.vector.engine_nop().then_inc(pairs_counted, 1)
            dve.wait_ge(counted, 1)
            link(nc.vector.tensor_tensor(cnt[:, :], bank[1][:, 0:E], base_row[:, :], ALU.subtract))
            link(nc.vector.tensor_scalar(ti[:, :], cnt[:, :], float(P - 1), None, ALU.add))
            link(nc.vector.tensor_single_scalar(ti[:, :], ti[:, :], P.bit_length() - 1, ALU.arith_shift_right))
            link(nc.vector.tensor_copy(cum[:, 0, :], ti[:, :]))
            for s, sh in enumerate((1, 2, 4)):
                link(nc.vector.tensor_copy(cum[:, s + 1, 0:sh], cum[:, s, 0:sh]))
                link(nc.vector.tensor_tensor(cum[:, s + 1, sh:E], cum[:, s, sh:E], cum[:, s, 0:E - sh], ALU.add))
            link(nc.vector.tensor_tensor(vrow[:, :], cum[:, 3, :], cum[:, 0, :], ALU.subtract))
            link(nc.vector.scalar_tensor_tensor(vrow[:, :], vrow[:, :], float(P), cnt[:, :], ALU.mult, ALU.add))
            link(nc.vector.scalar_tensor_tensor(vrow[:, :], eota[:, :], float(SPAN), vrow[:, :], ALU.mult, ALU.add))
            shape = [P, NJ, E]
            link(nc.vector.tensor_tensor(ge[:, :, :], jota[:, :].unsqueeze(2).to_broadcast(shape),
                                         cum[:, 3, :].unsqueeze(1).to_broadcast(shape), ALU.is_ge))
            link(nc.vector.tensor_reduce(tv[:, 0, :], ge[:, :, :], AX.X, ALU.add))
            link(nc.vector.tensor_tensor(ge[:, :, :], tv[:, 0, :].unsqueeze(2).to_broadcast(shape),
                                         eota[:, :].unsqueeze(1).to_broadcast(shape), ALU.is_equal))
            link(nc.vector.tensor_reduce(tv[:, 1, :], ge[:, :, :], AX.X, ALU.add))
            link(nc.vector.tensor_tensor(ge[:, :, :], ge[:, :, :], vrow[:, :].unsqueeze(1).to_broadcast(shape), ALU.mult))
            link(nc.vector.tensor_reduce(tv[:, 2, :], ge[:, :, :], AX.X, ALU.add))
            link(nc.vector.tensor_scalar(tv[:, 3, :], jota[:, :], -float(P), -float(DUMMY), ALU.mult, ALU.add))
            link(nc.vector.tensor_tensor(tv[:, 3, :], tv[:, 3, :], tv[:, 1, :], ALU.mult))
            link(nc.vector.tensor_tensor(tv[:, 3, :], tv[:, 3, :], tv[:, 2, :], ALU.add))
            link(nc.vector.tensor_scalar(table[:, 0, :], tv[:, 3, :], float(DUMMY), None, ALU.add))
            link(nc.vector.tensor_scalar(tv[:, 0, :], tv[:, 0, :], float(E - 1), None, ALU.min))
            link(nc.vector.tensor_scalar(table[:, 1, :], tv[:, 0, :], float(2 * C * D), None, ALU.mult))
            nc.vector.tensor_scalar(table[:, 2, :], tv[:, 0, :], float(D), None, ALU.mult).then_inc(tabled, 1)
            dve.wait_ge(tabled, 1)

            dve.wait_ge(b_in, 32)
            dve.wait_ge(sent[1], 16 * G * NTURN)

            def bias(j):
                ex = dve.value_load(table[0:1, 2, bass.ds(j, 1)], min_val=0, max_val=(E - 1) * D)
                dve.wait_ge(h_done, j + 1)
                dve.wait_ge(g_done, j)
                nc.vector.tensor_tensor(hid, bank[1][:, :], keys[:, bass.ds(ex, D)], ALU.add).then_inc(hb_done, 1)

            def finish(j, r):
                dve.wait_ge(y_done, j + 1)
                dve.wait_ge(res_ready, j + 1 + R)
                nc.vector.tensor_tensor(res[r], bank[3][:, :], res[r], ALU.add).then_inc(out_done, 1)

            bias(0)
            with dve.Fori(0, NJTURN - 1) as i:
                for r in range(R):
                    bias(i * R + r + 1)
                    finish(i * R + r, r)
            for r in range(R):
                j = NJ - R + r
                if j + 1 < NJ:
                    bias(j + 1)
                finish(j, r)

        @block.tensor
        def _(pe):
            mm = nc.tensor.matmul
            pe.wait_ge(consts, NCONST)

            def free(n):
                if n >= 8:
                    copied(pe, n - 8)

            pe.wait_ge(ld["bias"], 48)
            n = J_BIAS
            nc.tensor.transpose(bank[n % 8][:, 0:3 * C], brow12[:, :], ident[0:3 * C, 0:3 * C]).then_inc(pre_mm, 1)
            pe.wait_ge(ld["wg"], 16)
            n = J_GSUM
            for c in range(C):
                for e in range(C):
                    last = mm(bank[n % 8][:, E * c:E * (c + 1)], ones_f[:, :], wg_sb[:, e, :], start=(e == 0), stop=(e == C - 1))
            last.then_inc(pre_mm, 1)
            pe.wait_ge(ld["wk"], 16)
            pe.wait_ge(ld["wq"], 16)
            for k in range(C):
                n = J_KQ + k
                for e in range(C):
                    last = mm(bank[n % 8][:, :], wk_sb[:, e, P * k:P * (k + 1)], wq_sb[:, e, :],
                              start=(e == 0), stop=(e == C - 1))
                last.then_inc(pre_mm, 1)
            n = J_U
            free(n)
            copied(pe, J_BIAS)
            for k in range(C):
                for e in range(C):
                    last = mm(bank[n % 8][:, k:k + 1], wk_sb[:, e, P * k:P * (k + 1)], bcol[:, e:e + 1],
                              start=(e == 0), stop=(e == C - 1))
            last.then_inc(pre_mm, 1)
            pe.wait_ge(ld["ctx"], 16)
            for b in range(B):
                n = J_CTX + b
                free(n)
                for c in range(C):
                    last = nc.tensor.transpose(bank[n % 8][:, K * c:K * (c + 1)], ctx_nat[0:K, b, P * c:P * (c + 1)],
                                               ident[0:K, 0:K])
                last.then_inc(pre_mm, 1)
            pe.wait_ge(ld["wo"], 16)
            for k in range(C):
                n = J_WOT + k
                free(n)
                for c in range(C):
                    last = nc.tensor.transpose(bank[n % 8][:, P * c:P * (c + 1)], wo_sb[:, c, P * k:P * (k + 1)],
                                               ident[:, :])
                last.then_inc(pre_mm, 1)
            pe.wait_ge(ld["wv"], 16)
            for k in range(C):
                copied(pe, J_WOT + k)
            for k in range(C):
                n = J_OV + k
                free(n)
                for e in range(C):
                    last = mm(bank[n % 8][:, :], wv_sb[:, e, P * k:P * (k + 1)], woT[:, e, :],
                              start=(e == 0), stop=(e == C - 1))
                last.then_inc(pre_mm, 1)
            n = J_WOG
            free(n)
            copied(pe, J_GSUM)
            for c in range(C):
                for e in range(C):
                    last = mm(bank[n % 8][:, E * c:E * (c + 1)], wo_sb[:, e, P * c:P * (c + 1)], wg_mid[:, e, :],
                              start=(e == 0), stop=(e == C - 1))
            last.then_inc(pre_mm, 1)
            n = J_WVG
            free(n)
            copied(pe, J_WOG)
            for k in range(C):
                for e in range(C):
                    last = mm(bank[n % 8][:, E * k:E * (k + 1)], wv_sb[:, e, P * k:P * (k + 1)], wo_gate[:, e, :],
                              start=(e == 0), stop=(e == C - 1))
            last.then_inc(pre_mm, 1)
            for k in range(C):
                copied(pe, J_KQ + k)
            for b in range(B):
                copied(pe, J_CTX + b)
            copied(pe, J_U)
            for c in range(C):
                for h in range(2):
                    n = J_KEYS + 2 * c + h
                    free(n)
                    for k in range(C):
                        last = mm(bank[n % 8][:, 0:4 * K], kq[:, k, P * c:P * (c + 1)], ctxT[:, k, 4 * K * h:4 * K * (h + 1)],
                                  start=(k == 0), stop=(k == C - 1))
                    last.then_inc(pre_mm, 1)
            for h in range(2):
                n = J_KB + h
                free(n)
                for k in range(C):
                    last = mm(bank[n % 8][0:1, 0:4 * K], ucol[:, k:k + 1], ctxT[:, k, 4 * K * h:4 * K * (h + 1)],
                              start=(k == 0), stop=(k == C - 1))
                last.then_inc(pre_mm, 1)
            n = J_VB
            free(n)
            pe.wait_ge(dve_seq, 2)
            for e in range(C):
                last = mm(bank[n % 8][:, :], bv_bc[:, e, :], woT[:, e, :], start=(e == 0), stop=(e == C - 1))
            last.then_inc(pre_mm, 1)
            n = J_VGB
            free(n)
            for e in range(C):
                mm(bank[n % 8][:, 0:E], bv_bc[:, e, :], wo_gate[:, e, :], start=(e == 0), stop=False)
            for e in range(C):
                last = mm(bank[n % 8][:, 0:E], bo_cb[:, e, :], wg_mid[:, e, :], start=False, stop=(e == C - 1))
            last.then_inc(pre_mm, 1)
            for k in range(C):
                copied(pe, J_OV + k)
            copied(pe, J_WVG)
            for b in range(B):
                for m, (rhs, w) in enumerate(((ov, D), (wv_gate, E))):
                    n = J_VAL + 2 * b + m
                    free(n)
                    for k in range(C):
                        last = mm(bank[n % 8][0:K, 0:w], ctxT[:, k, K * b:K * (b + 1)], rhs[:, k, :],
                                  start=(k == 0), stop=(k == C - 1))
                    last.then_inc(pre_mm, 1)
            pe.wait_ge(pre_act, sum(1 for who in jobs if who == "act"))
            pe.wait_ge(pre_dve, sum(1 for who in jobs if who == "dve"))

            def transpose_x(t, j):
                pe.wait_ge(xn_ready, t + 1)
                need(pe, xT_done, t)
                for c in range(C):
                    last = nc.tensor.transpose(bank[0][:, P * c:P * (c + 1)], xn[j % 2][:, P * c:P * (c + 1)],
                                               ident[:, :])
                last.then_inc(tx_done, 1)

            def scores(t, j, b):
                pe.wait_ge(xT_done, t + 1)
                for c in range(C):
                    mm(bank[2 + j % 2][:, 0:P], xnT[:, c, :], keys[:, bass.ds((b * C + c) * P, P)],
                       start=(c == 0), stop=False)
                mm(bank[2 + j % 2][:, 0:P], ones_f[0:1, :], key_bias[:, bass.ds(b * P, P)],
                   start=False, stop=True).then_inc(s_done, 1)

            def transpose_p(t, j):
                pe.wait_ge(exp_done, t + 1)
                need(pe, x1_done, 2 * t - 3)
                nc.tensor.transpose(bank[4 + j % 2][0:K, 0:P], prob[j % 2], ident[:, :]).then_inc(pt_done, 1)

            def mix(t, j, b):
                pe.wait_ge(pT_done, t + 1)
                need(pe, x1_done, 2 * t - 2)
                mm(bank[4 + j % 2][:, P:P + E], probT[j % 2], val_gate[:, bass.ds(b * E, E)], start=True, stop=True)
                mm(bank[6 + j % 2][:, :], probT[j % 2], vals[0:K, bass.ds(b * D, D)], start=True, stop=True)\
                    .then_inc(pv_done, 1)

            def rank(n, g):
                pe.wait_ge(picked, n + 1)
                o = bank[1][:, 0:G * E]
                mm(o, before[:, :], pick[:, :, :].rearrange("p t e -> p (t e)"), start=True, stop=False)
                for q in range(G - 1):
                    mm(bank[1][:, E * (q + 1):E * G], ones_h[:, :], pick[:, q:q + 1, :].to_broadcast([P, G - 1 - q, E]),
                       start=False, stop=False)
                mm(o, ones_h[:, :], seen[:, g:g + 1, :].to_broadcast([P, G, E]), start=False, stop=True)\
                    .then_inc(ranked, 1)

            def step(k, j, turn):
                if is_tile(k):
                    transpose_x(k, j)
                if is_tile(k - 1):
                    scores(k - 1, (j - 1) % U, 2 * turn + (j - 1) // G)
                if is_tile(k - 2):
                    transpose_p(k - 2, (j - 2) % U)
                if is_tile(k - 3):
                    mix(k - 3, (j - 3) % U, 2 * turn + (j - 3) // G)
                if j % G == 0 and is_tile(k - 8):
                    rank(2 * turn + (j - 8) // G, (j - 8) // G % 2)

            for k in range(U):
                step(k, k, 0)
            with pe.Fori(1, NTURN) as i:
                for j in range(U):
                    step(i * U + j, j, i)
            for k in range(NT, NT + U):
                step(k, k % U, k // U)

            pe.wait_ge(pairs_counted, 1)
            mm(bank[1][:, 0:E], ones_h[:, :], seen[:, 0, :], start=True, stop=True).then_inc(counted, 1)

            pe.wait_ge(tabled, 1)
            pe.wait_ge(w_in, 16 * 2 * E)

            def transpose_x2(j):
                pe.wait_ge(xn2_ready, j + 1)
                pe.wait_ge(x2T_done, j)
                for c in range(C):
                    last = nc.tensor.transpose(bank[0][:, P * c:P * (c + 1)], xn2[:, P * c:P * (c + 1)], ident[:, :])
                last.then_inc(tx2_done, 1)

            def up(j, ex):
                pe.wait_ge(x2T_done, j + 1)
                pe.wait_ge(hb_done, j)
                for c in range(C):
                    last = mm(bank[1][:, :], x2T[:, c, :], wall[:, bass.ds(ex + c * D, D)],
                              start=(c == 0), stop=(c == C - 1))
                last.then_inc(h_done, 1)

            def transpose_g(j):
                pe.wait_ge(g_done, j + 1)
                pe.wait_ge(gT_done, j)
                for c in range(C):
                    last = nc.tensor.transpose(bank[2][:, P * c:P * (c + 1)], gel[:, P * c:P * (c + 1)], ident[:, :])
                last.then_inc(tg_done, 1)

            def down(j, ex):
                pe.wait_ge(gT_done, j + 1)
                pe.wait_ge(out_done, j)
                for c in range(C):
                    last = mm(bank[3][:, :], gelT[:, c, :], wall[:, bass.ds(ex + (C + c) * D, D)],
                              start=(c == 0), stop=(c == C - 1))
                last.then_inc(y_done, 1)

            def expert(j):
                return pe.value_load(table[0:1, 1, bass.ds(j, 1)], min_val=0, max_val=(E - 1) * 2 * C * D)

            transpose_x2(0)
            up(0, expert(0))
            transpose_x2(1)
            transpose_g(0)
            with pe.Fori(1, NJ - 1) as j:
                up(j, expert(j))
                transpose_x2(j + 1)
                down(j - 1, expert(j - 1))
                transpose_g(j)
            up(NJ - 1, expert(NJ - 1))
            down(NJ - 2, expert(NJ - 2))
            transpose_g(NJ - 1)
            down(NJ - 1, expert(NJ - 1))


_INS = ["x", "ctx_1024", "L0_xattn_Wk", "L0_xattn_Wv", "L0_xattn_bv", "L0_xattn_Wq", "L0_xattn_bq", "L0_xattn_Wo",
        "L0_xattn_bo", "L0_ffn_Wg", "L0_ffn_bg", "L0_ffn_W1", "L0_ffn_b1", "L0_ffn_W2", "L0_ffn_b2"]


def kernel(**inputs):
    import numpy as np
    import concourse.bacc as bacc
    from concourse.bass_utils import run_bass_kernel_spmd

    nc = bacc.Bacc("TRN2", target_bir_lowering=False, num_devices=1)
    arrays, args = {}, []
    for name in _INS:
        a = np.ascontiguousarray(inputs[name])
        arrays[f"in_{name}"] = a
        args.append(nc.dram_tensor(f"in_{name}", a.shape, mybir.dt.from_np(a.dtype), kind="ExternalInput").ap())
    args.append(nc.dram_tensor("out_x", (B, S, D), F32, kind="ExternalOutput").ap())
    build(nc, *args)
    r = run_bass_kernel_spmd(nc, [arrays], core_ids=[0])
    return r.results[0]["out_x"]
```

```python
import concourse.bass as bass
from concourse import mybir
from contextlib import ExitStack

F32 = mybir.dt.float32
F16 = mybir.dt.float16
I32 = mybir.dt.int32
ALU = mybir.AluOpType
ACT = mybir.ActivationFunctionType
AX = mybir.AxisListType

P = 128
D = 512
C = D // P
B = 8
S = 512
K = 120
E = 8
T = B * S
EPS = 1e-5
SCALE = float(D) ** -0.5
NT = T // P
U = 8
G = 4
NTURN = NT // U
ROW = D + 4
SPAN = P + T
DUMMY = E * SPAN
NJ = (T + E * (P - 1)) // P
R = 3
NJTURN = NJ // R
OOB = T + 1
NW = 2 * C
WSCALE = 64.0
NEARLY = E - 2
GAP = 2
M = 2
NM = 4


def need(eng, sem, value):
    if not (isinstance(value, int) and value <= 0):
        eng.wait_ge(sem, value)


def wait_apart(eng, sem, value, waits):
    if isinstance(value, int):
        return need(eng, sem, value)
    eng.wait_ge(sem, value)
    eng.sem_inc(waits, 1)


class Count:

    def __init__(self, sem, base=0):
        self.sem, self.base, self.n = sem, base, 0

    def inc(self, ins):
        self.n += 1
        return ins.then_inc(self.sem, 1)

    @property
    def value(self):
        return self.base + self.n


def is_tile(t):
    return not isinstance(t, int) or 0 <= t < NT


def build(nc, x, ctx_in, Wk, Wv, bv, Wq, bq, Wo, bo, Wg, bg, W1, b1, W2, b2, out):
    x_rows = x.rearrange("b s d -> (b s) d")
    out_rows = out.rearrange("b s d -> (b s) d")
    routed = nc.dram_tensor("routed_rows", (E * SPAN + P, ROW), F32, kind="Internal").ap()

    ctx = ExitStack()
    with ctx:
        def sb(name, shape, dt=F32):
            return ctx.enter_context(nc.sbuf_tensor(name, shape, dt))

        def sem(name):
            return ctx.enter_context(nc.semaphore(name))

        wall = sb("expert_weights", [P, (E * NW + GAP) * D])
        w_split = wall[:, :].bitcast(F16)
        w_of = wall[:, GAP * D:].rearrange("p (e m n) -> p e m n", e=E, m=2)
        keys = sb("keys_then_b1", [P, B * C * P])
        vals = sb("values_then_b2", [P, B * D])
        work = sb("work", [P, U * ROW + 4 * D])
        key_bias = sb("key_bias_and_value_gates", [1 + E, B * P])
        val_gate = sb("value_gate_columns", [K, B * E])
        ident = sb("identity", [P, P])
        ones_f = sb("ones_f32", [P, P])
        ones_h = sb("ones_f16", [P, P], F16)
        before = sb("strictly_before", [P, P], F16)
        wg_sb = sb("gate_weights", [P, C, E])
        bg_bc = sb("gate_bias", [P, E])
        wg_mid = sb("gate_weights_centred", [P, C, E])
        vg_bias = sb("value_gate_bias", [P, E])
        base_row = sb("expert_base_rows", [P, E])
        first_pick = sb("first_pick_rank", [P, E])
        half = sb("minus_half", [P, NT])
        brow12 = sb("bias_rows", [3 * C, P])
        bcol = sb("bias_columns", [P, 3 * C])
        wo_gate = sb("wo_gate", [P, C, E])
        row_weights = sb("row_weights", [P, C, 1 + E])
        row_split = sb("row_weights_split", [P, 2, C, 1 + E], F16)
        stats = sb("stats", [P, U, 6])
        mv1 = sb("mean_var_x", [P, NT, 2])
        mv2 = sb("mean_var_x1", [P, U, 2])
        ve1 = sb("var_eps_x", [P, NT])
        ve2 = sb("var_eps_x1", [P, U])
        rstd1 = sb("rstd_x", [P, NT])
        std1 = sb("std_x", [P, NT])
        negm1 = sb("neg_mean_x", [P, NT])
        nmr1 = sb("neg_mean_rstd_x", [P, NT])
        negmax = sb("neg_row_max", [P, U])
        rowsum = sb("row_sums", [P, U])
        rinv = sb("row_sum_inverses", [P, U])
        za = sb("gate_from_x", [P, U, E])
        z = sb("gate_logits", [P, U, E])
        zs = sb("gate_logits_scaled", [P, G, E])
        zl = sb("gate_logits_biased", [P, G, E])
        zt = sb("gate_scratch", [P, G, E])
        zm = sb("gate_max", [P, G])
        pick = sb("expert_one_hot", [P, G, E], F16)
        picks = sb("group_picks", [P, E], F16)
        seen = sb("picks_seen", [P, 2, E], F16)
        slot_i = sb("slot_index", [P, U], I32)
        negj = sb("minus_tile_rows", [P, NJ])
        ti = sb("tiles_int", [P, E], I32)
        cum = sb("tiles_cumulated", [P, 4, E + 4])
        vrow = sb("last_tile_rows", [P, E])
        jota = sb("tile_numbers", [P, NJ])
        eota = sb("expert_numbers", [P, E])
        table = sb("tile_table", [P, 3, NJ], I32)

        rows = work[:, 0:U * ROW].rearrange("p (u r) -> p u r", u=U)
        rest = U * ROW
        xn = work[:, rest:rest + D]
        xnT = [work[:, rest + D * n:rest + D * (n + 1)].rearrange("p (c t) -> p c t", c=C) for n in (1, 2)]
        prob = [work[:, rest + 3 * D + P * n:rest + 3 * D + P * n + K] for n in range(2)]
        probT = [work[0:K, rest + 3 * D + 2 * P + P * n:rest + 3 * D + 2 * P + P * (n + 1)] for n in range(2)]
        ctx_nat = work[:, 0:B * D].rearrange("p (b n) -> p b n", b=B)
        kq = work[:, rest:rest + C * D].bitcast(F16).rearrange("p (h c n) -> p h c n", h=2, c=C)
        woT = work[:, 0:C * D].rearrange("p (c n) -> p c n", c=C)
        bv_bc, bo_cb = (work[:, C * D + D * n:C * D + D * (n + 1)].rearrange("p (c t) -> p c t", c=C) for n in range(2))
        val_bias = work[:, C * D + 2 * D:C * D + 3 * D]
        bo_bc = vals[:, (B - 1) * D:B * D]
        pad_row = vals[:, 0:ROW]
        xm = w_of[:, NEARLY - 2, :, :].rearrange("p m n -> p (m n)").rearrange("p (u n) -> p u n", u=M * NM)
        xs = w_of[:, E - 1, :, :].rearrange("p m n -> p (m n)").rearrange("p (u n) -> p u n", u=U)
        wk_sb, wq_sb = (w_of[:, 7, m, :].rearrange("p (c n) -> p c n", c=C) for m in range(2))
        wv_sb, wo_sb = (w_of[:, 5, m, :].rearrange("p (c n) -> p c n", c=C) for m in range(2))
        ov = w_of[:, 7, 1, :].bitcast(F16).rearrange("p (h c n) -> p h c n", h=2, c=C)
        ctxT = w_of[:, 6, :, :].rearrange("p m n -> p (m n)")[:, 0:C * B * K].bitcast(F16)\
            .rearrange("p (h c s) -> p h c s", h=2, c=C)
        at = [0]

        def carve(n):
            at[0] += n
            return work[:, at[0] - n:at[0]]

        rrow = [carve(ROW) for _ in range(R)]
        res = [carve(D) for _ in range(R)]
        xn2, x2T, hid, gel, gelT = (carve(D) for _ in range(5))
        ge = carve(NJ * E).rearrange("p (j e) -> p j e", j=NJ)
        tv = carve(4 * NJ).rearrange("p (v j) -> p v j", v=4)
        assert at[0] <= U * ROW + 4 * D
        x2T = x2T.bitcast(F16).rearrange("p (h c t) -> p h c t", h=2, c=C)
        gelT = gelT.bitcast(F16).rearrange("p (h c t) -> p h c t", h=2, c=C)
        out_id = sb("output_ids", [P, R], I32)

        bank = [ctx.enter_context(nc.psum_tensor(f"bank{n}", [P, D], F32)) for n in range(8)]

        ld = {n: sem(f"loaded_{n}") for n in ("wk", "wq", "ctx", "wv", "wo", "wg", "bias", "bo", "bg")}
        w_early = [sem(f"expert_{e}_loaded") for e in range(NEARLY)]
        w_late = sem("expert_6_loaded")
        w_last = [sem(f"last_expert_chunk_{n}_loaded") for n in range(NW)]
        high_done = sem("weights_hi_done")
        low_done = sem("weights_lo_done")
        b1_in = sem("b1_loaded")
        b2_in = sem("b2_loaded")
        pad_out = sem("pad_rows_written")
        consts = sem("constants_ready")
        pool_seq = sem("pool_sequence")
        dve_seq = sem("vector_sequence")
        pool_waits = sem("pool_waits_passed")
        dve_waits = sem("vector_waits_passed")
        pre_mm = sem("preparation_products")
        pre_act = sem("preparation_copies_act")
        rows_split = sem("row_weights_split_parts")
        pre_dve = sem("preparation_copies_dve")
        xg_in = [sem(f"x_group_loaded_{g}") for g in range(NM)]
        x_in = [sem(f"x_loaded_{u}") for u in range(U)]
        stats1 = sem("stats_of_x")
        scal1 = sem("scales_of_x")
        xn_ready = sem("xn_ready")
        tx_done = sem("xn_transposed")
        xT_done = sem("xnT_copied")
        s_done = sem("scores_done")
        s_read = sem("scores_read")
        exp_done = sem("exp_done")
        pt_done = sem("probs_transposed")
        pT_done = sem("probsT_copied")
        pv_done = sem("values_mixed")
        x1_done = sem("x1_done")
        stats2 = sem("stats_of_x1")
        scal2 = sem("logits_ready")
        picked = sem("experts_picked")
        ranked = sem("ranks_done")
        slotted = sem("slots_ready")
        sent = [sem(f"rows_routed_{u}") for u in range(U)]
        pairs_counted = sem("picks_all_seen")
        counted = sem("experts_counted")
        tabled = sem("tile_table_ready")
        row_in = [sem(f"row_tile_loaded_{r}") for r in range(R)]
        xn2_ready = sem("xn2_ready")
        res_ready = sem("residual_ready")
        tx2_done = sem("xn2_transposed")
        x2h_done = sem("xn2T_hi_copied")
        x2l_done = sem("xn2T_lo_done")
        h_done = sem("hidden_done")
        hb_done = sem("hidden_biased")
        g_done = sem("gelu_done")
        tg_done = sem("gelu_transposed")
        gh_done = sem("geluT_hi_copied")
        gl_done = sem("geluT_lo_done")
        y_done = sem("expert_product_done")
        out_done = sem("output_tile_ready")
        out_sent = [sem(f"output_sent_{r}") for r in range(R)]

        NCONST = 13

        jobs = []

        def job(eng, count=1):
            jobs.extend([eng] * count)
            return len(jobs) - count

        J_KQ = job("both", C)
        J_BIAS = job("dve")
        J_GSUM = job("dve")
        J_U = job("act")
        J_CTX = job("both", B)
        J_WOT = job("act", C)
        J_OV = job("both", C)
        J_WOG = job("act")
        J_WVG = job("act")
        J_KEYS = job("act", 2 * C)
        J_KB = job("act", 2)
        J_VB = job("dve")
        J_VGB = job("dve")
        J_VG = job("dve")
        J_VAL = job("dve", B)
        NJOBS = len(jobs)

        def copies(who, n=NJOBS - 1):
            return sum(1 for w in jobs[:n + 1] if w in (who, "both"))

        def copied(eng, n):
            if jobs[n] != "both":
                eng.wait_ge(pre_act if jobs[n] == "act" else pre_dve, copies(jobs[n], n))
            else:
                eng.wait_ge(pre_dve, copies("dve", n))

        block = ctx.enter_context(nc.Block())

        @block.sync
        def _(sp):
            def chunked(w):
                return w.rearrange("(c p) n -> p c n", p=P)

            def load_expert(e, loaded):
                for m, w in enumerate((W1, W2)):
                    sp.dma_start(wall[:, bass.ds((e * NW + m * C + GAP) * D, C * D)].rearrange("p (c n) -> p c n", c=C),
                                 w[bass.ds(e, 1)].rearrange("e (c p) n -> p (e c) n", p=P)).then_inc(loaded, 16)

            sp.dma_start(wk_sb, chunked(Wk)).then_inc(ld["wk"], 16)
            sp.dma_start(wq_sb, chunked(Wq)).then_inc(ld["wq"], 16)
            def load_group(n):
                g = n % NM
                need(sp, stats1, M * (n - NM + 1))
                sp.dma_start(xm[:, M * g:M * (g + 1), :],
                             x_rows[P * M * n:P * M * (n + 1), :].rearrange("(t p) d -> p t d", p=P)).then_inc(xg_in[g], 16)

            load_group(0)
            sp.dma_start(ctx_nat[0:K, :, :], ctx_in.rearrange("b k d -> k b d")).then_inc(ld["ctx"], 16)
            load_group(1)
            sp.dma_start(wo_sb, chunked(Wo)).then_inc(ld["wo"], 16)
            load_group(2)
            sp.dma_start(wv_sb, chunked(Wv)).then_inc(ld["wv"], 16)
            load_group(3)
            for n in range(NM, NT // M):
                if n % NM == 0 and n // NM <= NEARLY - 2:
                    load_expert(n // NM - 1, w_early[n // NM - 1])
                load_group(n)
            load_expert(3, w_early[3])
            sp.wait_ge(stats1, NT)
            load_expert(NEARLY - 2, w_early[NEARLY - 2])
            sp.wait_ge(pre_mm, J_WVG + 1)
            load_expert(NEARLY - 1, w_early[NEARLY - 1])

            def load_x(t, u):
                need(sp, x1_done, 2 * t - 2 * U + 2)
                sp.dma_start(xs[:, u, :], x_rows[bass.ds(t * P, P), :]).then_inc(x_in[u], 16)

            for u in range(U):
                if u == C:
                    sp.wait_ge(pre_mm, NJOBS)
                    sp.wait_ge(pre_dve, copies("dve"))
                load_x(u, u)
            load_expert(E - 2, w_late)
            with sp.Fori(1, NTURN) as i:
                for u in range(U):
                    load_x(i * U + u, u)
            for u in range(U):
                sp.wait_ge(x1_done, 2 * (NT - U + u) + 2)
                sp.dma_start(xs[:, u, :], chunked((W1, W2)[u // C][E - 1])[:, u % C, :]).then_inc(w_last[u], 16)
                if u == C:
                    sp.wait_ge(s_done, NT)
                    sp.dma_start(keys[:, :], b1.rearrange("e d -> (e d)").partition_broadcast(P)).then_inc(b1_in, 16)
            sp.wait_ge(pv_done, NT)
            for u in range(G):
                sp.wait_ge(sent[u], 16 * NTURN)
            sp.dma_start(vals[:, :], b2.rearrange("e d -> (e d)").partition_broadcast(P)).then_inc(b2_in, 16)
            for u in range(U):
                sp.wait_ge(sent[u], 16 * NTURN)
            sp.wait_ge(pad_out, 16 * (E + 1))
            sp.wait_ge(tabled, 1)
            with sp.Fori(0, NJTURN) as i:
                for r in range(R):
                    j = i * R + r
                    sp.wait_ge(res_ready, j + 1)
                    start = sp.value_load(table[0:1, 0, bass.ds(j, 1)], min_val=0, max_val=DUMMY)
                    sp.dma_start(rrow[r], routed[bass.ds(start, P), :]).then_inc(row_in[r], 16)

        @block.gpsimd
        def _(pool):
            seq = Count(pool_seq)

            def link(ins):
                seq.inc(ins)
                pool.wait_ge(pool_seq, seq.value)

            pool.sem_inc(res_ready, R)
            nc.gpsimd.memset(ones_f[:, :], 1.0).then_inc(consts, 1)
            nc.gpsimd.memset(ones_h[:, :], 1.0).then_inc(consts, 1)
            nc.gpsimd.memset(half[:, :], -0.5).then_inc(consts, 1)
            nc.gpsimd.memset(key_bias[:, :], 0.0).then_inc(consts, 1)
            nc.gpsimd.iota(seen[:, 0, :], pattern=[[SPAN // P, E]], base=1, channel_multiplier=0,
                           allow_small_or_imprecise_dtypes=True).then_inc(consts, 1)
            link(nc.gpsimd.memset(ident[:, :], 0.0))
            nc.gpsimd.affine_select(out=ident[:, :], in_=ident[:, :], compare_op=ALU.not_equal, fill=1.0, base=0,
                                    pattern=[[-1, P]], channel_multiplier=1).then_inc(consts, 1)
            link(nc.gpsimd.memset(before[:, :], 1.0))
            nc.gpsimd.affine_select(out=before[:, :], in_=before[:, :], compare_op=ALU.is_gt, fill=0.0, base=0,
                                    pattern=[[1, P]], channel_multiplier=-1).then_inc(consts, 1)
            nc.gpsimd.iota(base_row[:, :], pattern=[[SPAN, E]], base=P, channel_multiplier=0,
                           allow_small_or_imprecise_dtypes=True).then_inc(consts, 1)
            nc.gpsimd.iota(first_pick[:, :], pattern=[[-1, E]], base=E, channel_multiplier=0,
                           allow_small_or_imprecise_dtypes=True).then_inc(consts, 1)
            nc.gpsimd.iota(jota[:, :], pattern=[[1, NJ]], base=0, channel_multiplier=0,
                           allow_small_or_imprecise_dtypes=True).then_inc(consts, 1)
            nc.gpsimd.iota(negj[:, :], pattern=[[-P, NJ]], base=-P - DUMMY, channel_multiplier=0,
                           allow_small_or_imprecise_dtypes=True).then_inc(consts, 1)
            nc.gpsimd.memset(cum[:, :, :], 0.0).then_inc(consts, 1)
            nc.gpsimd.iota(eota[:, :], pattern=[[1, E]], base=0, channel_multiplier=0,
                           allow_small_or_imprecise_dtypes=True).then_inc(consts, 1)
            link(nc.gpsimd.memset(pad_row, 0.0))
            link(nc.gpsimd.memset(pad_row[:, D + 2:D + 3].bitcast(I32), OOB))
            ids = rows[:, :, D + 2].bitcast(I32)
            for e in range(E + 1):
                pool.dma_start(routed[SPAN * e:SPAN * e + P, :], pad_row).then_inc(pad_out, 16)
            pool.wait_ge(stats1, NT)
            link(nc.gpsimd.tensor_scalar(ve1[:, :], mv1[:, :, 1], EPS, 1.0, ALU.add, ALU.mult))
            link(nc.gpsimd.tensor_tensor(rstd1[:, :], ve1[:, :], half[:, :], ALU.pow))
            link(nc.gpsimd.tensor_scalar(negm1[:, :], mv1[:, :, 0], -1.0, 0.0, ALU.mult, ALU.add))
            nc.gpsimd.tensor_tensor(nmr1[:, :], negm1[:, :], rstd1[:, :], ALU.mult).then_inc(scal1, 1)
            nc.gpsimd.tensor_tensor(std1[:, :], ve1[:, :], rstd1[:, :], ALU.mult).then_inc(scal1, 1)
            pool.wait_ge(pre_mm, NJOBS)
            pool.wait_ge(pre_dve, copies("dve"))
            link(nc.gpsimd.iota(ids, pattern=[[P, U]], base=0, channel_multiplier=1))
            link(nc.gpsimd.memset(rows[:, :, D + 3], 0.0))

            def scale(c, n, g):
                gs = slice(G * g, G * (g + 1))
                wait_apart(pool, stats2, n + 1, pool_waits)
                c.inc(nc.gpsimd.tensor_scalar(ve2[:, gs], mv2[:, gs, 1], EPS, 1.0, ALU.add, ALU.mult))
                wait_apart(pool, pool_seq, c.value, pool_waits)
                c.inc(nc.gpsimd.tensor_tensor(rows[:, gs, D + 1], ve2[:, gs], half[:, 0:G], ALU.pow))
                wait_apart(pool, pool_seq, c.value, pool_waits)
                c.inc(nc.gpsimd.tensor_tensor(zs[:, :, :], z[:, gs, :],
                                              rows[:, gs, D + 1].unsqueeze(2).to_broadcast([P, G, E]), ALU.mult))
                wait_apart(pool, pool_seq, c.value, pool_waits)
                nc.gpsimd.tensor_tensor(zl[:, :, :], zs[:, :, :], bg_bc[:, :].unsqueeze(1).to_broadcast([P, G, E]),
                                        ALU.add).then_inc(scal2, 1)
                c.inc(nc.gpsimd.tensor_scalar(rows[:, gs, D], mv2[:, gs, 0], -1.0, 0.0, ALU.mult, ALU.add))
                wait_apart(pool, pool_seq, c.value, pool_waits)

            def route(n, g):
                wait_apart(pool, slotted, n + 1, pool_waits)
                for j in range(G * g, G * (g + 1)):
                    pool.indirect_dma_start(routed, bass.IndirectOffsetOnAxis(ap=slot_i[:, j:j + 1], axis=0),
                                            rows[:, j, :], None).then_inc(sent[j], 16)

            def renumber(c, i, g):
                gs = slice(G * g, G * (g + 1))
                for j in range(G * g, G * (g + 1)):
                    wait_apart(pool, sent[j], i * 16 + 16, pool_waits)
                c.inc(nc.gpsimd.tensor_scalar(ids[:, gs], ids[:, gs], float(P * U), 1.0, ALU.add, ALU.mult))
                wait_apart(pool, pool_seq, c.value, pool_waits)

            pool.wait_ge(ld["bg"], 16)
            def route_turn(c, i):
                scale(c, 2 * i, 0)
                if not isinstance(i, int):
                    renumber(c, i - 1, 1)
                route(2 * i, 0)
                scale(c, 2 * i + 1, 1)
                renumber(c, i, 0)
                route(2 * i + 1, 1)

            route_turn(seq, 0)
            per_turn = 2 * 5
            start = seq.value
            with pool.Fori(1, NTURN) as i:
                c = Count(pool_seq, start + (i - 1) * per_turn)
                route_turn(c, i)
                assert c.n == per_turn

            pool.wait_ge(b2_in, 16)

            def normalise(j, r, turn):
                wait_apart(pool, row_in[r], 16 * turn + 16, pool_waits)
                wait_apart(pool, tx2_done, j, pool_waits)
                nc.gpsimd.tensor_scalar(xn2, rrow[r][:, 0:D], rrow[r][:, D:D + 1], rrow[r][:, D + 1:D + 2],
                                        ALU.add, ALU.mult).then_inc(xn2_ready, 1)
                wait_apart(pool, out_sent[r], 16 * turn, pool_waits)
                ex = pool.value_load(table[0:1, 2, bass.ds(j, 1)], min_val=0, max_val=(E - 1) * D)
                nc.gpsimd.tensor_copy(out_id[:, r:r + 1], rrow[r][:, D + 2:D + 3].bitcast(I32))
                nc.gpsimd.tensor_tensor(res[r], rrow[r][:, 0:D], vals[:, bass.ds(ex, D)],
                                        ALU.add).then_inc(res_ready, 1)

            def send(j, r):
                wait_apart(pool, out_done, j + 1, pool_waits)
                pool.indirect_dma_start(out_rows, bass.IndirectOffsetOnAxis(ap=out_id[:, r:r + 1], axis=0),
                                        res[r], None, bounds_check=T - 1, oob_is_err=False).then_inc(out_sent[r], 16)

            for j in range(R):
                normalise(j, j, 0)
                if j >= 2:
                    send(j - 2, j - 2)
            with pool.Fori(1, NJTURN) as i:
                for r in range(R):
                    j = i * R + r
                    normalise(j, r, i)
                    send(j - 2, (r - 2) % R)
            for j in (NJ - 2, NJ - 1):
                send(j, j % R)
            for r in range(R):
                pool.wait_ge(out_sent[r], 16 * NJTURN)

        @block.scalar
        def _(act):
            chunk_rows = "(c p) -> c p"
            act.dma_start(brow12[0:C, :], bq.rearrange(chunk_rows, p=P)).then_inc(ld["bias"], 16)
            act.dma_start(brow12[C:2 * C, :], bv.rearrange(chunk_rows, p=P)).then_inc(ld["bias"], 16)
            act.dma_start(brow12[2 * C:3 * C, :], bo.rearrange(chunk_rows, p=P)).then_inc(ld["bias"], 16)
            act.dma_start(wg_sb[:, :, :], Wg.rearrange("(c p) e -> p c e", p=P)).then_inc(ld["wg"], 16)
            act.dma_start(bo_bc, bo.partition_broadcast(P)).then_inc(ld["bo"], 16)
            act.dma_start(bg_bc[:, :], bg.partition_broadcast(P)).then_inc(ld["bg"], 16)

            def copy(n, dst, src, scale=1.0):
                assert jobs[n] in ("act", "both")
                act.wait_ge(pre_mm, n + 1)
                nc.scalar.activation(dst, src, ACT.Copy, scale=scale).then_inc(pre_act, 1)

            def high(n):
                need(act, low_done, n - GAP + 1)
                nc.scalar.activation(w_split[:, bass.ds(n * 2 * D, D)], wall[:, bass.ds((n + GAP) * D, D)],
                                     ACT.Copy, scale=WSCALE).then_inc(high_done, 1)

            for k in range(C):
                n = J_KQ + k
                copy(n, kq[:, 0, k, :], bank[n % 8][:, :], WSCALE)
            n = J_U
            copy(n, row_weights[:, :, 0], bank[n % 8][:, 0:C], SCALE)
            for b in range(B):
                n = J_CTX + b
                copy(n, ctxT[:, 0, :, K * b:K * (b + 1)], bank[n % 8][:, 0:C * K].rearrange("p (c s) -> p c s", c=C))
            for k in range(C):
                n = J_WOT + k
                copy(n, woT[:, k, :], bank[n % 8][:, :])
            for k in range(C):
                n = J_OV + k
                copy(n, ov[:, 0, k, :], bank[n % 8][:, :], WSCALE)
                if k == 0:
                    act.wait_ge(w_early[0], 32)
                for m in range(2):
                    high(2 * k + m)
            for n, dst in ((J_WOG, wo_gate), (J_WVG, row_weights[:, :, 1:1 + E])):
                copy(n, dst[:, :, :], bank[n % 8][:, 0:C * E].rearrange("p (c e) -> p c e", c=C))
            act.wait_ge(pre_act, copies("act", J_WVG))
            nc.scalar.activation(row_split[:, 0, :, :], row_weights[:, :, :], ACT.Copy, scale=WSCALE)\
                .then_inc(rows_split, 1)
            act.wait_ge(w_early[1], 32)
            for n in range(NW, 2 * NW):
                high(n)
            for m in range(2 * C):
                n = J_KEYS + m
                c, h = m // 2, m % 2
                dst = keys[:, :].rearrange("p (b c k) -> p b c k", b=B, c=C)[:, 4 * h:4 * h + 4, c, 0:K]
                copy(n, dst, bank[n % 8][:, 0:4 * K].rearrange("p (b k) -> p b k", b=4), SCALE / WSCALE)
                if m % C == 0:
                    act.wait_ge(w_early[2 + m // C], 32)
                for q in range(2):
                    high(2 * NW + 2 * m + q)
            act.wait_ge(consts, NCONST)
            for h in range(2):
                n = J_KB + h
                copy(n, key_bias[:, :].rearrange("o (b k) -> o b k", b=B)[:, 4 * h:4 * h + 4, 0:K],
                     bank[n % 8][0:1 + E, 0:4 * K].rearrange("p (b k) -> p b k", b=4), 1.0 / WSCALE)
            for e in range(NEARLY - 2, NEARLY):
                act.wait_ge(w_early[e], 32)
                for n in range(e * NW, (e + 1) * NW):
                    high(n)

            def normalise(t, j, turn):
                act.wait_ge(x_in[j], turn * 16 + 16)
                need(act, tx_done, t)
                nc.scalar.activation(xn, xs[:, j, :], ACT.Identity, bias=nmr1[:, bass.ds(t, 1)],
                                     scale=rstd1[:, bass.ds(t, 1)]).then_inc(xn_ready, 1)

            def xT(t, j):
                act.wait_ge(tx_done, t + 1)
                need(act, s_done, t - 1)
                nc.scalar.activation(xnT[j % 2], bank[0][:, :].rearrange("p (c t) -> p c t", c=C),
                                     ACT.Copy).then_inc(xT_done, 1)

            def exp(t, j):
                act.wait_ge(s_read, 2 * t + 2)
                need(act, pt_done, t - 1)
                nc.scalar.activation(prob[j % 2], bank[2 + j % 2][:, 0:K], ACT.Exp, bias=negmax[:, j:j + 1],
                                     accum_out=rowsum[:, j:j + 1]).then_inc(exp_done, 1)

            def pT(t, j):
                act.wait_ge(pt_done, t + 1)
                need(act, pv_done, t - 1)
                nc.scalar.activation(probT[j % 2], bank[4 + j % 2][0:K, 0:P], ACT.Copy).then_inc(pT_done, 1)

            def step(k, j, turn):
                if is_tile(k):
                    xT(k, j)
                if is_tile(k + 1):
                    normalise(k + 1, (j + 1) % U, turn + (j + 1) // U)
                if is_tile(k - 1):
                    exp(k - 1, (j - 1) % U)
                if is_tile(k - 2):
                    pT(k - 2, (j - 2) % U)

            act.wait_ge(scal1, 2)
            act.wait_ge(pre_mm, NJOBS)
            for k in range(-1, U - 1):
                step(k, k % U, k // U)
            act.wait_ge(w_late, 32)
            with act.Fori(1, NTURN) as i:
                for j in range(U):
                    step(i * U + j - 1, (j - 1) % U, i + (j - 1) // U)
                    if j % G == G - 1:
                        high(NEARLY * NW + 2 * (i - 1) + j // G)
            for n in range(NEARLY * NW + 2 * (NTURN - 1), E * NW):
                k = NT - 1 + n - (NEARLY * NW + 2 * (NTURN - 1))
                if k < NT + 2:
                    step(k, k % U, k // U)
                if n >= (E - 1) * NW:
                    act.wait_ge(w_last[n % NW], 16)
                high(n)

            nc.scalar.activation(rinv[:, 0:1], half[:, 0:1], ACT.Gelu)
            for u in range(U):
                act.wait_ge(sent[u], 16 * NTURN)

            def x2T_high(j):
                act.wait_ge(tx2_done, j + 1)
                act.wait_ge(h_done, j)
                nc.scalar.activation(x2T[:, 0, :, :], bank[0][:, :].rearrange("p (c t) -> p c t", c=C),
                                     ACT.Copy).then_inc(x2h_done, 1)

            def gelu(j):
                act.wait_ge(hb_done, j + 1)
                act.wait_ge(tg_done, j)
                nc.scalar.activation(gel, hid, ACT.Gelu).then_inc(g_done, 1)

            def gT_high(j):
                act.wait_ge(tg_done, j + 1)
                act.wait_ge(y_done, j)
                nc.scalar.activation(gelT[:, 0, :, :], bank[2][:, :].rearrange("p (c t) -> p c t", c=C),
                                     ACT.Copy).then_inc(gh_done, 1)

            x2T_high(0)
            gelu(0)
            x2T_high(1)
            gT_high(0)
            with act.Fori(1, NJ - 1) as j:
                x2T_high(j + 1)
                gelu(j)
                gT_high(j)
            gelu(NJ - 1)
            gT_high(NJ - 1)

        @block.vector
        def _(dve):
            seq = Count(dve_seq)

            def link(ins):
                seq.inc(ins)
                dve.wait_ge(dve_seq, seq.value)


            def ready(n):
                assert jobs[n] == "dve"
                dve.wait_ge(pre_mm, n + 1)

            def low_part(n, a, src, scale=1.0):
                assert jobs[n] == "both"
                dve.wait_ge(pre_act, copies("act", n))
                nc.vector.scalar_tensor_tensor(a[1], src, scale, a[0], ALU.mult, ALU.subtract).then_inc(pre_dve, 1)

            def moments_of_x(n):
                dve.wait_ge(xg_in[n % NM], 16 * (n // NM + 1))
                for u in range(M):
                    seq.inc(nc.vector.bn_stats(stats[:, u, :], xm[:, M * (n % NM) + u, :]))
                dve.wait_ge(dve_seq, seq.value)
                for u in range(M):
                    nc.vector.bn_aggr(mv1[:, M * n + u, :], stats[:, u, :]).then_inc(stats1, 1)
                dve.wait_ge(stats1, M * (n + 1))

            moments_of_x(0)
            for k in range(C):
                n = J_KQ + k
                low_part(n, [kq[:, h, k, :] for h in range(2)], bank[n % 8][:, :], WSCALE)
                if k == 1:
                    moments_of_x(1)
            n = J_BIAS
            ready(n)
            nc.vector.tensor_copy(bcol[:, :], bank[n % 8][:, 0:3 * C]).then_inc(pre_dve, 1)
            dve.wait_ge(pre_dve, copies("dve", J_BIAS))
            n = J_GSUM
            ready(n)
            dve.wait_ge(ld["wg"], 16)
            nc.vector.scalar_tensor_tensor(wg_mid[:, :, :], bank[n % 8][:, 0:E].unsqueeze(1).to_broadcast([P, C, E]),
                                           -1.0 / D, wg_sb[:, :, :], ALU.mult, ALU.add).then_inc(pre_dve, 1)
            for b in range(B):
                n = J_CTX + b
                low_part(n, [ctxT[:, h, :, K * b:K * (b + 1)] for h in range(2)],
                     bank[n % 8][:, 0:C * K].rearrange("p (c s) -> p c s", c=C))

            def low(n):
                dve.wait_ge(high_done, n + 1)
                nc.vector.scalar_tensor_tensor(w_split[:, bass.ds(n * 2 * D + D, D)], wall[:, bass.ds((n + GAP) * D, D)],
                                               WSCALE, w_split[:, bass.ds(n * 2 * D, D)], ALU.mult,
                                               ALU.subtract).then_inc(low_done, 1)

            at_group = [0] * 6 + [2] * 4 + [4] * 2 + [2] * 3 + [NW + 2]
            n_low = 0
            for n in range(2, NT // M):
                moments_of_x(n)
                if n == 5:
                    dve.wait_ge(pre_mm, J_CTX + B)
                    link(nc.vector.tensor_copy(bv_bc, bcol[:, C:2 * C].unsqueeze(2).to_broadcast([P, C, P])))
                    link(nc.vector.tensor_copy(bo_cb, bcol[:, 2 * C:3 * C].unsqueeze(2).to_broadcast([P, C, P])))
                    k = 0
                    low_part(J_OV + k, [ov[:, h, k, :] for h in range(2)], bank[(J_OV + k) % 8][:, :], WSCALE)
                if 6 <= n < 6 + C - 1:
                    k = n - 5
                    low_part(J_OV + k, [ov[:, h, k, :] for h in range(2)], bank[(J_OV + k) % 8][:, :], WSCALE)
                for m in range(at_group[n]):
                    low(n_low + m)
                    if n == 10 and m == 0:
                        dve.wait_ge(rows_split, 1)
                        nc.vector.scalar_tensor_tensor(row_split[:, 1, :, :], row_weights[:, :, :], WSCALE,
                                                       row_split[:, 0, :, :], ALU.mult, ALU.subtract)\
                            .then_inc(rows_split, 1)
                n_low += at_group[n]
            assert n_low == (NEARLY - 2) * NW
            keys4 = keys[:, :].rearrange("p (b c k) -> p b c k", b=B, c=C)
            for c in range(C):
                link(nc.vector.tensor_copy(keys4[:, :, c, K:P], wg_mid[:, c:c + 1, :].to_broadcast([P, B, E])))
            n = J_VB
            ready(n)
            dve.wait_ge(ld["bo"], 16)
            nc.vector.tensor_tensor(val_bias, bank[n % 8][:, :], bo_bc, ALU.add).then_inc(pre_dve, 1)
            n = J_VGB
            ready(n)
            nc.vector.tensor_copy(vg_bias[:, :], bank[n % 8][:, 0:E]).then_inc(pre_dve, 1)
            dve.wait_ge(pre_dve, copies("dve", J_VGB))
            n = J_VG
            ready(n)
            nc.vector.tensor_tensor(val_gate[:, :].rearrange("p (b e) -> p b e", b=B),
                                    bank[n % 8][0:K, 0:B * (1 + E)].rearrange("p (b e) -> p b e", b=B)[:, :, 1:1 + E],
                                    vg_bias[0:K, :].unsqueeze(1).to_broadcast([K, B, E]), ALU.add).then_inc(pre_dve, 1)
            dve.wait_ge(pad_out, 16 * (E + 1))
            for b in range(B):
                n = J_VAL + b
                ready(n)
                nc.vector.scalar_tensor_tensor(vals[0:K, D * b:D * (b + 1)], bank[n % 8][0:K, :], 1.0 / WSCALE,
                                               val_bias[0:K, :], ALU.mult, ALU.add).then_inc(pre_dve, 1)
                for m in range(2):
                    low((NEARLY - 2) * NW + 2 * b + m)

            dve.wait_ge(ld["bg"], 16)
            dve.wait_ge(scal1, 2)

            def pick_experts(c, n, g):
                def link(ins):
                    c.inc(ins)
                    dve.wait_ge(dve_seq, c.value)

                def over_e(a):
                    return a.unsqueeze(2).to_broadcast([P, G, E])

                def over_t(a):
                    return a.unsqueeze(1).to_broadcast([P, G, E])

                dve.wait_ge(scal2, n + 1)
                link(nc.vector.tensor_reduce(zm[:, :], zl[:, :, :], AX.X, ALU.max))
                link(nc.vector.tensor_tensor(zt[:, :, :], zl[:, :, :], over_e(zm[:, :]), ALU.is_equal))
                link(nc.vector.tensor_tensor(zt[:, :, :], zt[:, :, :], over_t(first_pick[:, :]), ALU.mult))
                link(nc.vector.tensor_reduce(zm[:, :], zt[:, :, :], AX.X, ALU.max))
                nc.vector.tensor_tensor(pick[:, :, :], over_t(first_pick[:, :]), over_e(zm[:, :]),
                                        ALU.is_equal).then_inc(picked, 1)

            def place(c, n, g):
                gs = slice(G * g, G * (g + 1))

                def link(ins):
                    c.inc(ins)
                    dve.wait_ge(dve_seq, c.value)

                dve.wait_ge(ranked, n + 1)
                link(nc.vector.tensor_tensor(zt[:, :, :], bank[1][:, 0:G * E].rearrange("p (t e) -> p t e", t=G),
                                             pick[:, :, :], ALU.mult))
                with nc.allow_low_precision(reason="row numbers and counts below 64 are exact"):
                    nc.vector.tensor_reduce(slot_i[:, gs], zt[:, :, :], AX.X, ALU.add).then_inc(slotted, 1)
                    link(nc.vector.tensor_reduce(picks[:, :], pick[:, :, :].rearrange("p t e -> p e t"), AX.X,
                                                 ALU.add))
                link(nc.vector.tensor_tensor(seen[:, 1 - g, :], seen[:, g, :], picks[:, :], ALU.add))

            def read_scores(t, j):
                dve.wait_ge(s_done, t + 1)
                nc.vector.tensor_scalar(za[:, j, :], bank[2 + j % 2][:, K:P], std1[:, bass.ds(t, 1)], None,
                                        ALU.mult).then_inc(s_read, 1)
                nc.vector.tensor_reduce(negmax[:, j:j + 1], bank[2 + j % 2][:, 0:K], AX.X, ALU.max,
                                        negate=True).then_inc(s_read, 1)

            def moments(c, t, j):
                dve.wait_ge(x1_done, 2 * t + 2)
                c.inc(nc.vector.bn_stats(stats[:, j, :], rows[:, j, 0:D]))
                return c.value

            def mean_var(c, j, taken):
                wait_apart(dve, dve_seq, taken, dve_waits)
                ins = nc.vector.bn_aggr(mv2[:, j, :], stats[:, j, :])
                if j % G == G - 1:
                    ins.then_inc(stats2, 1)
                else:
                    c.inc(ins)

            def mixed(c, t, j, turn):
                if j % G > 0:
                    taken = moments(c, t - 1, j - 1)
                dve.wait_ge(exp_done, t + 1)
                c.inc(nc.vector.reciprocal(rinv[:, j:j + 1], rowsum[:, j:j + 1]))
                dve.wait_ge(dve_seq, c.value)
                dve.wait_ge(pv_done, t + 1)
                nc.vector.scalar_tensor_tensor(z[:, j, :], bank[4 + j % 2][:, P:P + E], rinv[:, j:j + 1],
                                               za[:, j, :], ALU.mult, ALU.add).then_inc(x1_done, 1)
                need(dve, sent[j], 16 * turn)
                nc.vector.scalar_tensor_tensor(rows[:, j, 0:D], bank[6 + j % 2][:, :], rinv[:, j:j + 1],
                                               xs[:, j, :], ALU.mult, ALU.add).then_inc(x1_done, 1)
                if j % G > 0:
                    mean_var(c, j - 1, taken)
                if j % G == G - 1:
                    mean_var(c, j, moments(c, t, j))

            def step(c, k, j, turn):
                if j % G == 1 and is_tile(k - 9):
                    place(c, 2 * turn + (j - 9) // G, (j - 9) // G % 2)
                if is_tile(k - 1):
                    read_scores(k - 1, (j - 1) % U)
                if is_tile(k - 3):
                    mixed(c, k - 3, (j - 3) % U, turn if j >= 3 else turn - 1)
                if j % G == G - 1 and is_tile(k - 7):
                    pick_experts(c, 2 * turn + (j - 7) // G, (j - 7) // G % 2)

            for k in range(U):
                step(seq, k, k, 0)
            per_turn = U + 2 * U - 2 + 2 * (4 + 3)
            start = seq.value
            with dve.Fori(1, NTURN) as i:
                c = Count(dve_seq, start + i * per_turn - per_turn)
                for j in range(U):
                    step(c, i * U + j, j, i)
                    if j % G == G - 1:
                        low(NEARLY * NW + 2 * (i - 1) + j // G)
                assert c.n == per_turn, c.n
            c = Count(dve_seq, start + (NTURN - 1) * per_turn)
            n_low = NEARLY * NW + 2 * (NTURN - 1)
            for k in range(NT, NT + U):
                step(c, k, k % U, k // U)
                for n in range((1, 1, 3, 1, 0, 0, 0, 0)[k - NT]):
                    low(n_low)
                    n_low += 1

            def link(ins):
                c.inc(ins)
                dve.wait_ge(dve_seq, c.value)

            nc.vector.engine_nop().then_inc(pairs_counted, 1)
            dve.wait_ge(counted, 1)
            end_row = bank[1][:, 0:E]
            link(nc.vector.scalar_tensor_tensor(ti[:, :], end_row, float(P - 1), base_row[:, :], ALU.add, ALU.subtract))
            link(nc.vector.tensor_single_scalar(ti[:, :], ti[:, :], P.bit_length() - 1, ALU.arith_shift_right))
            link(nc.vector.tensor_copy(cum[:, 0, 4:], ti[:, :]))
            for s, sh in enumerate((1, 2, 4)):
                link(nc.vector.tensor_tensor(cum[:, s + 1, 4:], cum[:, s, 4:], cum[:, s, 4 - sh:4 - sh + E], ALU.add))
            link(nc.vector.tensor_tensor(vrow[:, :], cum[:, 3, 4:], cum[:, 0, 4:], ALU.subtract))
            link(nc.vector.scalar_tensor_tensor(vrow[:, :], vrow[:, :], float(P), end_row, ALU.mult, ALU.add))
            shape = [P, NJ, E]
            link(nc.vector.tensor_tensor(ge[:, :, :], jota[:, :].unsqueeze(2).to_broadcast(shape),
                                         cum[:, 3:4, 4:].to_broadcast(shape), ALU.is_ge))
            link(nc.vector.tensor_reduce(tv[:, 0, :], ge[:, :, :], AX.X, ALU.add))
            link(nc.vector.tensor_tensor(ge[:, :, :], tv[:, 0, :].unsqueeze(2).to_broadcast(shape),
                                         eota[:, :].unsqueeze(1).to_broadcast(shape), ALU.is_equal))
            link(nc.vector.tensor_reduce(tv[:, 1, :], ge[:, :, :], AX.X, ALU.add))
            link(nc.vector.tensor_tensor(ge[:, :, :], ge[:, :, :], vrow[:, :].unsqueeze(1).to_broadcast(shape), ALU.mult))
            link(nc.vector.tensor_reduce(tv[:, 2, :], ge[:, :, :], AX.X, ALU.add))
            link(nc.vector.tensor_tensor(tv[:, 1, :], negj[:, :], tv[:, 1, :], ALU.mult))
            link(nc.vector.scalar_tensor_tensor(table[:, 0, :], tv[:, 1, :], float(DUMMY), tv[:, 2, :], ALU.add, ALU.add))
            for n, width in ((1, NW * 2 * D), (2, D)):
                ins = nc.vector.tensor_scalar(table[:, n, :], tv[:, 0, :], float(E - 1), float(width), ALU.min, ALU.mult)
                if n == 1:
                    link(ins)
                else:
                    ins.then_inc(tabled, 1)
            dve.wait_ge(tabled, 1)
            for n in range(n_low, E * NW):
                low(n)

            dve.wait_ge(b1_in, 16)
            for u in range(U):
                dve.wait_ge(sent[u], 16 * NTURN)

            def bias(j):
                ex = dve.value_load(table[0:1, 2, bass.ds(j, 1)], min_val=0, max_val=(E - 1) * D)
                dve.wait_ge(h_done, j + 1)
                dve.wait_ge(g_done, j)
                nc.vector.scalar_tensor_tensor(hid, bank[1][:, :], 1.0 / WSCALE, keys[:, bass.ds(ex, D)], ALU.mult,
                                               ALU.add).then_inc(hb_done, 1)

            def x2T_low(j):
                dve.wait_ge(x2h_done, j + 1)
                nc.vector.tensor_tensor(x2T[:, 1, :, :], bank[0][:, :].rearrange("p (c t) -> p c t", c=C),
                                        x2T[:, 0, :, :], ALU.subtract).then_inc(x2l_done, 1)

            def gT_low(j):
                dve.wait_ge(gh_done, j + 1)
                nc.vector.tensor_tensor(gelT[:, 1, :, :], bank[2][:, :].rearrange("p (c t) -> p c t", c=C),
                                        gelT[:, 0, :, :], ALU.subtract).then_inc(gl_done, 1)

            def finish(j, r):
                dve.wait_ge(y_done, j + 1)
                dve.wait_ge(res_ready, j + 1 + R)
                nc.vector.scalar_tensor_tensor(res[r], bank[3][:, :], 1.0 / WSCALE, res[r], ALU.mult,
                                               ALU.add).then_inc(out_done, 1)

            def step(j, r):
                if not isinstance(j, int) or j + 1 < NJ:
                    bias(j + 1)
                if not isinstance(j, int) or j + 2 < NJ:
                    x2T_low(j + 2)
                finish(j, r)
                if not isinstance(j, int) or j + 1 < NJ:
                    gT_low(j + 1)

            x2T_low(0)
            bias(0)
            x2T_low(1)
            gT_low(0)
            with dve.Fori(0, NJTURN - 1) as i:
                for r in range(R):
                    step(i * R + r, r)
            for r in range(R):
                step(NJ - R + r, r)

        @block.tensor
        def _(pe):
            mm = nc.tensor.matmul
            PARTS = ((0, 0), (0, 1), (1, 0))

            def free(n):
                if n >= 8:
                    copied(pe, n - 8)

            pe.wait_ge(ld["wk"], 16)
            pe.wait_ge(ld["wq"], 16)
            for k in range(C):
                n = J_KQ + k
                for e in range(C):
                    last = mm(bank[n % 8][:, :], wk_sb[:, e, P * k:P * (k + 1)], wq_sb[:, e, :],
                              start=(e == 0), stop=(e == C - 1))
                last.then_inc(pre_mm, 1)
            pe.wait_ge(consts, NCONST)
            pe.wait_ge(ld["bias"], 48)
            n = J_BIAS
            nc.tensor.transpose(bank[n % 8][:, 0:3 * C], brow12[:, :], ident[0:3 * C, 0:3 * C]).then_inc(pre_mm, 1)
            pe.wait_ge(ld["wg"], 16)
            n = J_GSUM
            for e in range(C):
                last = mm(bank[n % 8][:, 0:E], ones_f[:, :], wg_sb[:, e, :], start=(e == 0), stop=(e == C - 1))
            last.then_inc(pre_mm, 1)
            n = J_U
            copied(pe, J_BIAS)
            for k in range(C):
                for e in range(C):
                    last = mm(bank[n % 8][:, k:k + 1], wk_sb[:, e, P * k:P * (k + 1)], bcol[:, e:e + 1],
                              start=(e == 0), stop=(e == C - 1))
            last.then_inc(pre_mm, 1)
            pe.wait_ge(ld["ctx"], 16)
            for b in range(B):
                n = J_CTX + b
                free(n)
                for c in range(C):
                    last = nc.tensor.transpose(bank[n % 8][:, K * c:K * (c + 1)], ctx_nat[0:K, b, P * c:P * (c + 1)],
                                               ident[0:K, 0:K])
                last.then_inc(pre_mm, 1)
            pe.wait_ge(ld["wo"], 16)
            for k in range(C):
                n = J_WOT + k
                free(n)
                for c in range(C):
                    last = nc.tensor.transpose(bank[n % 8][:, P * c:P * (c + 1)], wo_sb[:, c, P * k:P * (k + 1)],
                                               ident[:, :])
                last.then_inc(pre_mm, 1)
            pe.wait_ge(ld["wv"], 16)
            for k in range(C):
                copied(pe, J_WOT + k)
            for k in range(C):
                n = J_OV + k
                free(n)
                for e in range(C):
                    last = mm(bank[n % 8][:, :], wv_sb[:, e, P * k:P * (k + 1)], woT[:, e, :],
                              start=(e == 0), stop=(e == C - 1))
                last.then_inc(pre_mm, 1)
            n = J_WOG
            free(n)
            copied(pe, J_GSUM)
            for c in range(C):
                for e in range(C):
                    last = mm(bank[n % 8][:, E * c:E * (c + 1)], wo_sb[:, e, P * c:P * (c + 1)], wg_mid[:, e, :],
                              start=(e == 0), stop=(e == C - 1))
            last.then_inc(pre_mm, 1)
            n = J_WVG
            free(n)
            copied(pe, J_WOG)
            for k in range(C):
                for e in range(C):
                    last = mm(bank[n % 8][:, E * k:E * (k + 1)], wv_sb[:, e, P * k:P * (k + 1)], wo_gate[:, e, :],
                              start=(e == 0), stop=(e == C - 1))
            last.then_inc(pre_mm, 1)
            for k in range(C):
                copied(pe, J_KQ + k)
            for b in range(B):
                copied(pe, J_CTX + b)
            copied(pe, J_U)
            for c in range(C):
                for h in range(2):
                    n = J_KEYS + 2 * c + h
                    free(n)
                    for k in range(C):
                        for u, v in PARTS:
                            last = mm(bank[n % 8][:, 0:4 * K], kq[:, u, k, P * c:P * (c + 1)],
                                      ctxT[:, v, k, 4 * K * h:4 * K * (h + 1)],
                                      start=(k == 0 and u + v == 0), stop=(k == C - 1 and u == 1))
                    last.then_inc(pre_mm, 1)
            pe.wait_ge(rows_split, 2)
            for h in range(2):
                n = J_KB + h
                free(n)
                for k in range(C):
                    for u, v in PARTS:
                        last = mm(bank[n % 8][0:1 + E, 0:4 * K], row_split[:, u, k, :],
                                  ctxT[:, v, k, 4 * K * h:4 * K * (h + 1)],
                                  start=(k == 0 and u + v == 0), stop=(k == C - 1 and u == 1))
                last.then_inc(pre_mm, 1)
            n = J_VB
            free(n)
            pe.wait_ge(dve_seq, 6 * M + 2)
            for e in range(C):
                last = mm(bank[n % 8][:, :], bv_bc[:, e, :], woT[:, e, :], start=(e == 0), stop=(e == C - 1))
            last.then_inc(pre_mm, 1)
            n = J_VGB
            free(n)
            for e in range(C):
                mm(bank[n % 8][:, 0:E], bv_bc[:, e, :], wo_gate[:, e, :], start=(e == 0), stop=False)
            for e in range(C):
                last = mm(bank[n % 8][:, 0:E], bo_cb[:, e, :], wg_mid[:, e, :], start=False, stop=(e == C - 1))
            last.then_inc(pre_mm, 1)
            n = J_VG
            free(n)
            for h in range(2):
                copied(pe, J_KB + h)
            for b in range(B):
                last = nc.tensor.transpose(bank[n % 8][0:K, (1 + E) * b:(1 + E) * (b + 1)], key_bias[:, P * b:P * b + K],
                                           ident[0:1 + E, 0:1 + E])
            last.then_inc(pre_mm, 1)
            for k in range(C):
                copied(pe, J_OV + k)
            for b in range(B):
                n = J_VAL + b
                free(n)
                for k in range(C):
                    for u, v in PARTS:
                        last = mm(bank[n % 8][0:K, :], ctxT[:, u, k, K * b:K * (b + 1)], ov[:, v, k, :],
                                  start=(k == 0 and u + v == 0), stop=(k == C - 1 and u == 1))
                last.then_inc(pre_mm, 1)
            pe.wait_ge(pre_act, copies("act"))
            pe.wait_ge(pre_dve, copies("dve"))

            def transpose_x(t, j):
                pe.wait_ge(xn_ready, t + 1)
                need(pe, xT_done, t)
                for c in range(C):
                    last = nc.tensor.transpose(bank[0][:, P * c:P * (c + 1)], xn[:, P * c:P * (c + 1)], ident[:, :])
                last.then_inc(tx_done, 1)

            def scores(t, j, b):
                pe.wait_ge(xT_done, t + 1)
                for c in range(C):
                    mm(bank[2 + j % 2][:, 0:P], xnT[j % 2][:, c, :], keys[:, bass.ds((b * C + c) * P, P)],
                       start=(c == 0), stop=False)
                mm(bank[2 + j % 2][:, 0:P], ones_f[0:1, :], key_bias[0:1, bass.ds(b * P, P)],
                   start=False, stop=True).then_inc(s_done, 1)

            def transpose_p(t, j):
                pe.wait_ge(exp_done, t + 1)
                need(pe, x1_done, 2 * t - 3)
                nc.tensor.transpose(bank[4 + j % 2][0:K, 0:P], prob[j % 2], ident[:, :]).then_inc(pt_done, 1)

            def mix(t, j, b):
                pe.wait_ge(pT_done, t + 1)
                need(pe, x1_done, 2 * t - 2)
                mm(bank[4 + j % 2][:, P:P + E], probT[j % 2], val_gate[:, bass.ds(b * E, E)], start=True, stop=True)
                mm(bank[6 + j % 2][:, :], probT[j % 2], vals[0:K, bass.ds(b * D, D)], start=True, stop=True)\
                    .then_inc(pv_done, 1)

            def rank(n, g):
                pe.wait_ge(picked, n + 1)
                o = bank[1][:, 0:G * E]
                mm(o, before[:, :], pick[:, :, :].rearrange("p t e -> p (t e)"), start=True, stop=False)
                for q in range(G - 1):
                    mm(bank[1][:, E * (q + 1):E * G], ones_h[:, :], pick[:, q:q + 1, :].to_broadcast([P, G - 1 - q, E]),
                       start=False, stop=False)
                mm(o, ones_h[:, :], seen[:, g:g + 1, :].to_broadcast([P, G, E]), start=False, stop=True)\
                    .then_inc(ranked, 1)

            def step(k, j, turn):
                if is_tile(k):
                    transpose_x(k, j)
                if is_tile(k - 1):
                    scores(k - 1, (j - 1) % U, 2 * turn + (j - 1) // G)
                if is_tile(k - 2):
                    transpose_p(k - 2, (j - 2) % U)
                if is_tile(k - 3):
                    mix(k - 3, (j - 3) % U, 2 * turn + (j - 3) // G)
                if j % G == 0 and is_tile(k - 8):
                    rank(2 * turn + (j - 8) // G, (j - 8) // G % 2)

            for k in range(U):
                step(k, k, 0)
            with pe.Fori(1, NTURN) as i:
                for j in range(U):
                    step(i * U + j, j, i)
            for k in range(NT, NT + U):
                step(k, k % U, k // U)

            pe.wait_ge(pairs_counted, 1)
            mm(bank[1][:, 0:E], ones_h[:, :], seen[:, 0, :], start=True, stop=True).then_inc(counted, 1)

            pe.wait_ge(tabled, 1)
            pe.wait_ge(low_done, E * NW)

            def transpose_x2(j):
                pe.wait_ge(xn2_ready, j + 1)
                pe.wait_ge(x2l_done, j)
                for c in range(C):
                    last = nc.tensor.transpose(bank[0][:, P * c:P * (c + 1)], xn2[:, P * c:P * (c + 1)], ident[:, :])
                last.then_inc(tx2_done, 1)

            def product(o, a, first, low_ready, j):
                for c in range(C):
                    for h in range(2):
                        mm(o, a[:, 0, c, :], w_split[:, bass.ds(first + (2 * c + h) * D, D)],
                           start=(c == 0 and h == 0), stop=False)
                pe.wait_ge(low_ready, j + 1)
                for c in range(C):
                    last = mm(o, a[:, 1, c, :], w_split[:, bass.ds(first + 2 * c * D, D)], start=False, stop=(c == C - 1))
                return last

            def up(j, ex):
                pe.wait_ge(x2h_done, j + 1)
                pe.wait_ge(hb_done, j)
                product(bank[1][:, :], x2T, ex, x2l_done, j).then_inc(h_done, 1)

            def transpose_g(j):
                pe.wait_ge(g_done, j + 1)
                pe.wait_ge(gl_done, j)
                for c in range(C):
                    last = nc.tensor.transpose(bank[2][:, P * c:P * (c + 1)], gel[:, P * c:P * (c + 1)], ident[:, :])
                last.then_inc(tg_done, 1)

            def down(j, ex):
                pe.wait_ge(gh_done, j + 1)
                pe.wait_ge(out_done, j)
                product(bank[3][:, :], gelT, ex + C * 2 * D, gl_done, j).then_inc(y_done, 1)

            def experts(j, n):
                return nc.values_load_multi_w_load_instructions(
                    table[0:1, 1, bass.ds(j, n)], engines=[mybir.EngineType.PE], min_val=0,
                    max_val=(E - 1) * NW * 2 * D,
                    skip_runtime_bounds_check_because="the table is made from expert numbers held to E - 1")[1]

            transpose_x2(0)
            up(0, experts(0, 1)[0])
            transpose_x2(1)
            transpose_g(0)
            def step(j, ex, ex_before):
                up(j, ex)
                transpose_x2(j + 1)
                down(j - 1, ex_before)
                transpose_g(j)

            assert (NJ - 3) % R == 0
            with pe.Fori(0, (NJ - 3) // R) as i:
                ex = experts(i * R, R + 1)
                for r in range(1, R + 1):
                    step(i * R + r, ex[r], ex[r - 1])
            ex = experts(NJ - 3, 3)
            step(NJ - 2, ex[1], ex[0])
            up(NJ - 1, ex[2])
            down(NJ - 2, ex[1])
            transpose_g(NJ - 1)
            down(NJ - 1, ex[2])


_INS = ["x", "ctx_1024", "L0_xattn_Wk", "L0_xattn_Wv", "L0_xattn_bv", "L0_xattn_Wq", "L0_xattn_bq", "L0_xattn_Wo",
        "L0_xattn_bo", "L0_ffn_Wg", "L0_ffn_bg", "L0_ffn_W1", "L0_ffn_b1", "L0_ffn_W2", "L0_ffn_b2"]


def kernel(**inputs):
    import numpy as np
    import concourse.bacc as bacc
    from concourse.bass_utils import run_bass_kernel_spmd

    nc = bacc.Bacc("TRN2", target_bir_lowering=False, num_devices=1)
    arrays, args = {}, []
    for name in _INS:
        a = np.ascontiguousarray(inputs[name])
        arrays[f"in_{name}"] = a
        args.append(nc.dram_tensor(f"in_{name}", a.shape, mybir.dt.from_np(a.dtype), kind="ExternalInput").ap())
    args.append(nc.dram_tensor("out_x", (B, S, D), F32, kind="ExternalOutput").ap())
    build(nc, *args)
    r = run_bass_kernel_spmd(nc, [arrays], core_ids=[0])
    return r.results[0]["out_x"]
```

```python
import concourse.bass as bass
from concourse import mybir
from contextlib import ExitStack

F32 = mybir.dt.float32
F16 = mybir.dt.float16
I32 = mybir.dt.int32
ALU = mybir.AluOpType
ACT = mybir.ActivationFunctionType
AX = mybir.AxisListType

P = 128
D = 512
C = D // P
B = 8
S = 512
K = 120
E = 8
T = B * S
EM = E + 1
EPS = 1e-5
SCALE = float(D) ** -0.5
NT = T // P
U = 8
G = 4
NTURN = NT // U
ROW = D + 4
SPAN = P + T
DUMMY = E * SPAN
NJ = (T + E * (P - 1)) // P
R = 3
NJTURN = NJ // R
OOB = T + 1
NW = 2 * C
WSCALE = 64.0
NEARLY = E - 2
GAP = 2
M = 2
NM = 4


def need(eng, sem, value):
    if not (isinstance(value, int) and value <= 0):
        eng.wait_ge(sem, value)


def wait_apart(eng, sem, value, waits):
    if isinstance(value, int):
        return need(eng, sem, value)
    eng.wait_ge(sem, value)
    eng.sem_inc(waits, 1)


class Count:

    def __init__(self, sem, base=0):
        self.sem, self.base, self.n = sem, base, 0

    def inc(self, ins):
        self.n += 1
        return ins.then_inc(self.sem, 1)

    @property
    def value(self):
        return self.base + self.n


def is_tile(t):
    return not isinstance(t, int) or 0 <= t < NT


def build(nc, x, ctx_in, Wk, Wv, bv, Wq, bq, Wo, bo, Wg, bg, W1, b1, W2, b2, out):
    x_rows = x.rearrange("b s d -> (b s) d")
    out_rows = out.rearrange("b s d -> (b s) d")
    routed = nc.dram_tensor("routed_rows", (E * SPAN + P, ROW), F32, kind="Internal").ap()

    ctx = ExitStack()
    with ctx:
        def sb(name, shape, dt=F32):
            return ctx.enter_context(nc.sbuf_tensor(name, shape, dt))

        def sem(name):
            return ctx.enter_context(nc.semaphore(name))

        wall = sb("expert_weights", [P, (E * NW + GAP) * D])
        w_split = wall[:, :].bitcast(F16)
        w_of = wall[:, GAP * D:].rearrange("p (e m n) -> p e m n", e=E, m=2)
        keys = sb("keys_then_b1", [P, B * C * P])
        vals = sb("values_then_b2", [P, B * D])
        work = sb("work", [P, U * ROW + 4 * D])
        key_bias = sb("key_bias_and_value_gates", [1 + EM, B * P])
        val_gate = sb("value_gate_columns", [K, B * EM])
        bias_split = sb("key_bias_split", [1, 2, B * P], F16)
        ident = sb("identity", [P, P])
        ones_f = sb("ones_f32", [P, P])
        ones_h = sb("ones_f16", [P, P], F16)
        before = sb("strictly_before", [P, P], F16)
        wg_sb = sb("gate_weights", [P, C, E])
        bg_bc = sb("gate_bias", [P, E])
        wg_mid = sb("gate_weights_centred", [P, C, EM])
        vg_bias = sb("value_gate_bias", [P, EM])
        base_row = sb("expert_base_rows", [P, E])
        first_pick = sb("first_pick_rank", [P, E])
        half = sb("minus_half", [P, NT])
        brow12 = sb("bias_rows", [3 * C, P])
        bcol = sb("bias_columns", [P, 3 * C])
        wo_gate = sb("wo_gate", [P, C, EM])
        row_weights = sb("row_weights", [P, C, 1 + EM])
        row_split = sb("row_weights_split", [P, 2, C, 1 + EM], F16)
        stats = sb("stats", [P, U, 6])
        mv1 = sb("mean_var_x", [P, NT, 2])
        sum_sq = sb("square_sums_x1", [P, U])
        squares = sb("squares_unused", [P, D], mybir.dt.bfloat16)
        ve1 = sb("var_eps_x", [P, NT])
        ve2 = sb("var_eps_x1", [P, U])
        rstd1 = sb("rstd_x", [P, NT])
        std1 = sb("std_x", [P, NT])
        negm1 = sb("neg_mean_x", [P, NT])
        nmr1 = sb("neg_mean_rstd_x", [P, NT])
        negmax = sb("neg_row_max", [P, U])
        rowsum = sb("row_sums", [P, U])
        rinv = sb("row_sum_inverses", [P, U])
        za = sb("gate_and_mean_from_x", [P, NT * EM])
        z = sb("gate_and_mean", [P, U, EM])
        zs = sb("gate_logits_scaled", [P, G, E])
        zl = sb("gate_logits_biased", [P, G, E])
        zt = sb("gate_scratch", [P, G, E])
        zm = sb("gate_max", [P, G])
        pick = sb("expert_one_hot", [P, G, E], F16)
        picks = sb("group_picks", [P, E], F16)
        seen = sb("picks_seen", [P, 2, E], F16)
        slot_i = sb("slot_index", [P, U], I32)
        negj = sb("minus_tile_rows", [P, NJ])
        ti = sb("tiles_int", [P, E], I32)
        cum = sb("tiles_cumulated", [P, 4, E + 4])
        vrow = sb("last_tile_rows", [P, E])
        jota = sb("tile_numbers", [P, NJ])
        eota = sb("expert_numbers", [P, E])
        table = sb("tile_table", [P, 3, NJ], I32)

        rows = work[:, 0:U * ROW].rearrange("p (u r) -> p u r", u=U)
        rest = U * ROW
        xn = work[:, rest:rest + D]
        xnT = [work[:, rest + D * n:rest + D * (n + 1)].rearrange("p (c t) -> p c t", c=C) for n in (1, 2)]
        prob = [work[:, rest + 3 * D + P * n:rest + 3 * D + P * n + K] for n in range(2)]
        probT = [work[0:K, rest + 3 * D + 2 * P + P * n:rest + 3 * D + 2 * P + P * (n + 1)] for n in range(2)]
        ctx_nat = work[:, 0:B * D].rearrange("p (b n) -> p b n", b=B)
        kq = work[:, rest:rest + C * D].bitcast(F16).rearrange("p (h c n) -> p h c n", h=2, c=C)
        woT = work[:, 0:C * D].rearrange("p (c n) -> p c n", c=C)
        bv_bc, bo_cb = (work[:, C * D + D * n:C * D + D * (n + 1)].rearrange("p (c t) -> p c t", c=C) for n in range(2))
        val_bias = work[:, C * D + 2 * D:C * D + 3 * D]
        bo_bc = vals[:, (B - 1) * D:B * D]
        pad_row = vals[:, 0:ROW]
        xm = w_of[:, NEARLY - 2, :, :].rearrange("p m n -> p (m n)").rearrange("p (u n) -> p u n", u=M * NM)
        xs = w_of[:, E - 1, :, :].rearrange("p m n -> p (m n)").rearrange("p (u n) -> p u n", u=U)
        wk_sb, wq_sb = (w_of[:, 7, m, :].rearrange("p (c n) -> p c n", c=C) for m in range(2))
        wv_sb, wo_sb = (w_of[:, 5, m, :].rearrange("p (c n) -> p c n", c=C) for m in range(2))
        ov = w_of[:, 7, 1, :].bitcast(F16).rearrange("p (h c n) -> p h c n", h=2, c=C)
        ctxT = w_of[:, 6, :, :].rearrange("p m n -> p (m n)")[:, 0:C * B * K].bitcast(F16)\
            .rearrange("p (h c s) -> p h c s", h=2, c=C)
        at = [0]

        def carve(n):
            at[0] += n
            return work[:, at[0] - n:at[0]]

        rrow = [carve(ROW) for _ in range(R)]
        res = [carve(D) for _ in range(R)]
        xn2, x2T, hid, gel, gelT = (carve(D) for _ in range(5))
        ge = carve(NJ * E).rearrange("p (j e) -> p j e", j=NJ)
        tv = carve(4 * NJ).rearrange("p (v j) -> p v j", v=4)
        assert at[0] <= U * ROW + 4 * D
        x2T = x2T.bitcast(F16).rearrange("p (h c t) -> p h c t", h=2, c=C)
        gelT = gelT.bitcast(F16).rearrange("p (h c t) -> p h c t", h=2, c=C)
        out_id = sb("output_ids", [P, R], I32)

        bank = [ctx.enter_context(nc.psum_tensor(f"bank{n}", [P, D], F32)) for n in range(8)]

        ld = {n: sem(f"loaded_{n}") for n in ("ctx", "wv", "wo", "wg", "bias", "bo", "bg")}
        wkq_in = [sem(f"wk_wq_chunk_{c}_loaded") for c in range(C)]
        w_early = [sem(f"expert_{e}_loaded") for e in range(NEARLY)]
        w_late = sem("expert_6_loaded")
        w_last = [sem(f"last_expert_chunk_{n}_loaded") for n in range(NW)]
        high_done = sem("weights_hi_done")
        low_done = sem("weights_lo_done")
        b1_in = sem("b1_loaded")
        b2_in = sem("b2_loaded")
        pad_out = sem("pad_rows_written")
        consts = sem("constants_ready")
        pool_seq = sem("pool_sequence")
        dve_seq = sem("vector_sequence")
        pool_waits = sem("pool_waits_passed")
        pre_mm = sem("preparation_products")
        pre_act = sem("preparation_copies_act")
        rows_split = sem("row_weights_split_parts")
        bias_parts = sem("key_bias_split_parts")
        pre_dve = sem("preparation_copies_dve")
        xg_in = [sem(f"x_group_loaded_{g}") for g in range(NM)]
        x_in = [sem(f"x_loaded_{u}") for u in range(U)]
        stats1 = sem("stats_of_x")
        scal1 = sem("scales_of_x")
        xn_ready = sem("xn_ready")
        tx_done = sem("xn_transposed")
        xT_done = sem("xnT_copied")
        s_done = sem("scores_done")
        s_read = sem("scores_read")
        exp_done = sem("exp_done")
        pt_done = sem("probs_transposed")
        pT_done = sem("probsT_copied")
        pv_done = sem("values_mixed")
        x1_done = sem("x1_done")
        stats2 = sem("stats_of_x1")
        scal2 = sem("logits_ready")
        picked = sem("experts_picked")
        ranked = sem("ranks_done")
        slotted = sem("slots_ready")
        sent = [sem(f"rows_routed_{u}") for u in range(U)]
        pairs_counted = sem("picks_all_seen")
        counted = sem("experts_counted")
        tabled = sem("tile_table_ready")
        row_in = [sem(f"row_tile_loaded_{r}") for r in range(R)]
        xn2_ready = sem("xn2_ready")
        res_ready = sem("residual_ready")
        tx2_done = sem("xn2_transposed")
        x2h_done = sem("xn2T_hi_copied")
        x2l_done = sem("xn2T_lo_done")
        h_done = sem("hidden_done")
        hb_done = sem("hidden_biased")
        g_done = sem("gelu_done")
        tg_done = sem("gelu_transposed")
        gh_done = sem("geluT_hi_copied")
        gl_done = sem("geluT_lo_done")
        y_done = sem("expert_product_done")
        out_done = sem("output_tile_ready")
        out_sent = [sem(f"output_sent_{r}") for r in range(R)]

        NCONST = 14

        jobs = []

        def job(eng, count=1):
            jobs.extend([eng] * count)
            return len(jobs) - count

        J_KQ = job("both", C)
        J_BIAS = job("dve")
        J_GSUM = job("dve")
        J_CTX = job("both", B)
        J_WOT = job("act", C)
        J_OV = job("both", C)
        J_U = job("act")
        J_WOG = job("act")
        J_KEYS = [job("act") for _ in range(C)]
        J_WVG = job("act")
        J_KEYS += [job("act") for _ in range(C)]
        J_VB = job("dve")
        J_VGB = job("dve")
        J_KB = job("act", 2)
        J_VG = job("dve")
        J_VAL = job("dve", B)
        NJOBS = len(jobs)

        def copies(who, n=NJOBS - 1):
            return sum(1 for w in jobs[:n + 1] if w in (who, "both"))

        def copied(eng, n):
            if jobs[n] != "both":
                eng.wait_ge(pre_act if jobs[n] == "act" else pre_dve, copies(jobs[n], n))
            else:
                eng.wait_ge(pre_dve, copies("dve", n))

        block = ctx.enter_context(nc.Block())

        @block.sync
        def _(sp):
            def chunked(w):
                return w.rearrange("(c p) n -> p c n", p=P)

            def load_expert(e, loaded):
                for m, w in enumerate((W1, W2)):
                    sp.dma_start(wall[:, bass.ds((e * NW + m * C + GAP) * D, C * D)].rearrange("p (c n) -> p c n", c=C),
                                 w[bass.ds(e, 1)].rearrange("e (c p) n -> p (e c) n", p=P)).then_inc(loaded, 16)

            for c in range(C):
                sp.dma_start(wk_sb[:, c, :], chunked(Wk)[:, c, :]).then_inc(wkq_in[c], 16)
                sp.dma_start(wq_sb[:, c, :], chunked(Wq)[:, c, :]).then_inc(wkq_in[c], 16)
            def load_group(n):
                g = n % NM
                need(sp, stats1, M * (n - NM + 1))
                sp.dma_start(xm[:, M * g:M * (g + 1), :],
                             x_rows[P * M * n:P * M * (n + 1), :].rearrange("(t p) d -> p t d", p=P)).then_inc(xg_in[g], 16)

            load_group(0)
            sp.dma_start(ctx_nat[0:K, :, :], ctx_in.rearrange("b k d -> k b d")).then_inc(ld["ctx"], 16)
            load_group(1)
            sp.dma_start(wo_sb, chunked(Wo)).then_inc(ld["wo"], 16)
            load_group(2)
            sp.dma_start(wv_sb, chunked(Wv)).then_inc(ld["wv"], 16)
            load_group(3)
            for n in range(NM, NT // M):
                if n % NM == 0 and n // NM <= NEARLY - 2:
                    load_expert(n // NM - 1, w_early[n // NM - 1])
                load_group(n)
            load_expert(3, w_early[3])
            sp.wait_ge(stats1, NT)
            load_expert(NEARLY - 2, w_early[NEARLY - 2])
            sp.wait_ge(pre_mm, J_WVG + 1)
            load_expert(NEARLY - 1, w_early[NEARLY - 1])

            def load_x(t, u):
                need(sp, x1_done, 2 * t - 2 * U + 2)
                sp.dma_start(xs[:, u, :], x_rows[bass.ds(t * P, P), :]).then_inc(x_in[u], 16)

            for u in range(U):
                if u == C:
                    sp.wait_ge(pre_mm, NJOBS)
                    sp.wait_ge(pre_dve, copies("dve"))
                load_x(u, u)
            load_expert(E - 2, w_late)
            with sp.Fori(1, NTURN) as i:
                for u in range(U):
                    load_x(i * U + u, u)
            for u in range(U):
                sp.wait_ge(x1_done, 2 * (NT - U + u) + 2)
                sp.dma_start(xs[:, u, :], chunked((W1, W2)[u // C][E - 1])[:, u % C, :]).then_inc(w_last[u], 16)
                if u == C:
                    sp.wait_ge(s_done, NT)
                    sp.dma_start(keys[:, :], b1.rearrange("e d -> (e d)").partition_broadcast(P)).then_inc(b1_in, 16)
            sp.wait_ge(tabled, 1)
            def first_row(j):
                return sp.value_load(table[0:1, 0, bass.ds(j, 1)], min_val=0, max_val=DUMMY)

            def load_rows(j, r, start):
                sp.wait_ge(res_ready, j + 1)
                sp.dma_start(rrow[r], routed[bass.ds(start, P), :]).then_inc(row_in[r], 16)

            starts = [first_row(r) for r in range(R)]
            for u in range(U):
                sp.wait_ge(sent[u], 16 * NTURN)
            sp.wait_ge(pad_out, 16 * (E + 1))
            for r in range(R):
                load_rows(r, r, starts[r])
            sp.wait_ge(pv_done, NT)
            sp.dma_start(vals[:, :], b2.rearrange("e d -> (e d)").partition_broadcast(P)).then_inc(b2_in, 16)
            with sp.Fori(1, NJTURN) as i:
                for r in range(R):
                    load_rows(i * R + r, r, first_row(i * R + r))

        @block.gpsimd
        def _(pool):
            seq = Count(pool_seq)

            def link(ins):
                seq.inc(ins)
                pool.wait_ge(pool_seq, seq.value)

            pool.sem_inc(res_ready, R)
            nc.gpsimd.memset(ones_f[:, :], 1.0).then_inc(consts, 1)
            nc.gpsimd.memset(ones_h[:, :], 1.0).then_inc(consts, 1)
            nc.gpsimd.memset(half[:, :], -0.5).then_inc(consts, 1)
            nc.gpsimd.memset(key_bias[:, :], 0.0).then_inc(consts, 1)
            nc.gpsimd.iota(seen[:, 0, :], pattern=[[SPAN // P, E]], base=1, channel_multiplier=0,
                           allow_small_or_imprecise_dtypes=True).then_inc(consts, 1)
            link(nc.gpsimd.memset(ident[:, :], 0.0))
            nc.gpsimd.affine_select(out=ident[:, :], in_=ident[:, :], compare_op=ALU.not_equal, fill=1.0, base=0,
                                    pattern=[[-1, P]], channel_multiplier=1).then_inc(consts, 1)
            link(nc.gpsimd.memset(before[:, :], 1.0))
            nc.gpsimd.affine_select(out=before[:, :], in_=before[:, :], compare_op=ALU.is_gt, fill=0.0, base=0,
                                    pattern=[[1, P]], channel_multiplier=-1).then_inc(consts, 1)
            nc.gpsimd.iota(base_row[:, :], pattern=[[SPAN, E]], base=P, channel_multiplier=0,
                           allow_small_or_imprecise_dtypes=True).then_inc(consts, 1)
            nc.gpsimd.iota(first_pick[:, :], pattern=[[-1, E]], base=E, channel_multiplier=0,
                           allow_small_or_imprecise_dtypes=True).then_inc(consts, 1)
            nc.gpsimd.iota(jota[:, :], pattern=[[1, NJ]], base=0, channel_multiplier=0,
                           allow_small_or_imprecise_dtypes=True).then_inc(consts, 1)
            nc.gpsimd.iota(negj[:, :], pattern=[[-P, NJ]], base=-P - DUMMY, channel_multiplier=0,
                           allow_small_or_imprecise_dtypes=True).then_inc(consts, 1)
            nc.gpsimd.memset(cum[:, :, :], 0.0).then_inc(consts, 1)
            nc.gpsimd.memset(wg_mid[:, :, E], -1.0 / D).then_inc(consts, 1)
            nc.gpsimd.iota(eota[:, :], pattern=[[1, E]], base=0, channel_multiplier=0,
                           allow_small_or_imprecise_dtypes=True).then_inc(consts, 1)
            link(nc.gpsimd.memset(pad_row, 0.0))
            link(nc.gpsimd.memset(pad_row[:, D + 2:D + 3].bitcast(I32), OOB))
            ids = rows[:, :, D + 2].bitcast(I32)
            for e in range(E + 1):
                pool.dma_start(routed[SPAN * e:SPAN * e + P, :], pad_row).then_inc(pad_out, 16)
            pool.wait_ge(stats1, NT)
            link(nc.gpsimd.tensor_scalar(ve1[:, :], mv1[:, :, 1], EPS, 1.0, ALU.add, ALU.mult))
            link(nc.gpsimd.tensor_tensor(rstd1[:, :], ve1[:, :], half[:, :], ALU.pow))
            link(nc.gpsimd.tensor_scalar(negm1[:, :], mv1[:, :, 0], -1.0, 0.0, ALU.mult, ALU.add))
            nc.gpsimd.tensor_scalar(za[:, :].rearrange("p (t e) -> p t e", t=NT)[:, :, E], negm1[:, :], 1.0, 0.0, ALU.mult,
                                    ALU.add).then_inc(scal1, 1)
            nc.gpsimd.tensor_tensor(nmr1[:, :], negm1[:, :], rstd1[:, :], ALU.mult).then_inc(scal1, 1)
            nc.gpsimd.tensor_tensor(std1[:, :], ve1[:, :], rstd1[:, :], ALU.mult).then_inc(scal1, 1)
            pool.wait_ge(pre_mm, NJOBS)
            pool.wait_ge(pre_dve, copies("dve"))
            link(nc.gpsimd.iota(ids, pattern=[[P, U]], base=0, channel_multiplier=1))
            link(nc.gpsimd.memset(rows[:, :, D + 3], 0.0))

            def scale(c, n, g):
                gs = slice(G * g, G * (g + 1))
                wait_apart(pool, stats2, G * n + G, pool_waits)
                c.inc(nc.gpsimd.tensor_scalar(ve2[:, gs], sum_sq[:, gs], 1.0 / D, EPS, ALU.mult, ALU.add))
                wait_apart(pool, pool_seq, c.value, pool_waits)
                c.inc(nc.gpsimd.tensor_tensor(rows[:, gs, D + 1], ve2[:, gs], half[:, 0:G], ALU.pow))
                wait_apart(pool, pool_seq, c.value, pool_waits)
                c.inc(nc.gpsimd.tensor_scalar(rows[:, gs, D], z[:, gs, E], 1.0, 0.0, ALU.mult, ALU.add))
                c.inc(nc.gpsimd.tensor_tensor(zs[:, :, :], z[:, gs, 0:E],
                                              rows[:, gs, D + 1].unsqueeze(2).to_broadcast([P, G, E]), ALU.mult))
                wait_apart(pool, pool_seq, c.value, pool_waits)
                nc.gpsimd.tensor_tensor(zl[:, :, :], zs[:, :, :], bg_bc[:, :].unsqueeze(1).to_broadcast([P, G, E]),
                                        ALU.add).then_inc(scal2, 1)
                wait_apart(pool, pool_seq, c.value, pool_waits)

            def route(n, g):
                wait_apart(pool, slotted, n + 1, pool_waits)
                for j in range(G * g, G * (g + 1)):
                    pool.indirect_dma_start(routed, bass.IndirectOffsetOnAxis(ap=slot_i[:, j:j + 1], axis=0),
                                            rows[:, j, :], None).then_inc(sent[j], 16)

            def renumber(c, i, g):
                gs = slice(G * g, G * (g + 1))
                for j in range(G * g, G * (g + 1)):
                    wait_apart(pool, sent[j], i * 16 + 16, pool_waits)
                c.inc(nc.gpsimd.tensor_scalar(ids[:, gs], ids[:, gs], float(P * U), 1.0, ALU.add, ALU.mult))
                wait_apart(pool, pool_seq, c.value, pool_waits)

            pool.wait_ge(ld["bg"], 16)
            def route_turn(c, i):
                scale(c, 2 * i, 0)
                if not isinstance(i, int):
                    renumber(c, i - 1, 0)
                    renumber(c, i - 1, 1)
                route(2 * i, 0)
                scale(c, 2 * i + 1, 1)
                route(2 * i + 1, 1)

            route_turn(seq, 0)
            per_turn = 2 * 5
            start = seq.value
            with pool.Fori(1, NTURN) as i:
                c = Count(pool_seq, start + (i - 1) * per_turn)
                route_turn(c, i)
                assert c.n == per_turn

            def xhat(j, r, turn):
                wait_apart(pool, row_in[r], 16 * turn + 16, pool_waits)
                wait_apart(pool, tx2_done, j, pool_waits)
                nc.gpsimd.tensor_scalar(xn2, rrow[r][:, 0:D], rrow[r][:, D:D + 1], rrow[r][:, D + 1:D + 2],
                                        ALU.add, ALU.mult).then_inc(xn2_ready, 1)

            def residual(j, r, turn):
                wait_apart(pool, out_sent[r], 16 * turn, pool_waits)
                ex = pool.value_load(table[0:1, 2, bass.ds(j, 1)], min_val=0, max_val=(E - 1) * D)
                nc.gpsimd.tensor_copy(out_id[:, r:r + 1], rrow[r][:, D + 2:D + 3].bitcast(I32))
                nc.gpsimd.tensor_tensor(res[r], rrow[r][:, 0:D], vals[:, bass.ds(ex, D)],
                                        ALU.add).then_inc(res_ready, 1)

            def send(j, r):
                wait_apart(pool, out_done, j + 1, pool_waits)
                pool.indirect_dma_start(out_rows, bass.IndirectOffsetOnAxis(ap=out_id[:, r:r + 1], axis=0),
                                        res[r], None, bounds_check=T - 1, oob_is_err=False).then_inc(out_sent[r], 16)

            xhat(0, 0, 0)
            xhat(1, 1, 0)
            pool.wait_ge(b2_in, 16)
            pool.wait_ge(tabled, 3)
            residual(0, 0, 0)
            residual(1, 1, 0)
            xhat(2, 2, 0)
            residual(2, 2, 0)
            xhat(3, 0, 1)
            send(0, 0)
            with pool.Fori(1, NJTURN - 1) as i:
                for r in range(R):
                    j = i * R + r
                    residual(j, r, i)
                    xhat(j + 1, (r + 1) % R, i + (r + 1) // R)
                    send(j - 2, (r - 2) % R)
            for r in range(R):
                j = NJ - R + r
                residual(j, r, NJTURN - 1)
                if j + 1 < NJ:
                    xhat(j + 1, r + 1, NJTURN - 1)
                send(j - 2, (r - 2) % R)
            for j in (NJ - 2, NJ - 1):
                send(j, j % R)
            for r in range(R):
                pool.wait_ge(out_sent[r], 16 * NJTURN)

        @block.scalar
        def _(act):
            chunk_rows = "(c p) -> c p"
            act.dma_start(brow12[0:C, :], bq.rearrange(chunk_rows, p=P)).then_inc(ld["bias"], 16)
            act.dma_start(brow12[C:2 * C, :], bv.rearrange(chunk_rows, p=P)).then_inc(ld["bias"], 16)
            act.dma_start(brow12[2 * C:3 * C, :], bo.rearrange(chunk_rows, p=P)).then_inc(ld["bias"], 16)
            act.dma_start(wg_sb[:, :, :], Wg.rearrange("(c p) e -> p c e", p=P)).then_inc(ld["wg"], 16)
            act.dma_start(bo_bc, bo.partition_broadcast(P)).then_inc(ld["bo"], 16)
            act.dma_start(bg_bc[:, :], bg.partition_broadcast(P)).then_inc(ld["bg"], 16)

            def copy(n, dst, src, scale=1.0):
                assert jobs[n] in ("act", "both")
                act.wait_ge(pre_mm, n + 1)
                nc.scalar.activation(dst, src, ACT.Copy, scale=scale).then_inc(pre_act, 1)

            def high(n):
                need(act, low_done, n - GAP + 1)
                nc.scalar.activation(w_split[:, bass.ds(n * 2 * D, D)], wall[:, bass.ds((n + GAP) * D, D)],
                                     ACT.Copy, scale=WSCALE).then_inc(high_done, 1)

            for k in range(C):
                n = J_KQ + k
                copy(n, kq[:, 0, k, :], bank[n % 8][:, :], WSCALE)
            for b in range(B):
                n = J_CTX + b
                copy(n, ctxT[:, 0, :, K * b:K * (b + 1)], bank[n % 8][:, 0:C * K].rearrange("p (c s) -> p c s", c=C))
            for k in range(C):
                n = J_WOT + k
                copy(n, woT[:, k, :], bank[n % 8][:, :])
            for k in range(C):
                n = J_OV + k
                copy(n, ov[:, 0, k, :], bank[n % 8][:, :], WSCALE)
                if k == 0:
                    act.wait_ge(w_early[0], 32)
                if k == C - 1:
                    n = J_U
                    copy(n, row_weights[:, :, 0], bank[n % 8][:, 0:C], SCALE)
                    n = J_WOG
                    copy(n, wo_gate[:, :, :], bank[n % 8][:, 0:C * EM].rearrange("p (c e) -> p c e", c=C))
                for m in range(2):
                    high(2 * k + m)
            act.wait_ge(w_early[1], 32)
            for n in range(NW, 2 * NW):
                high(n)
            for m in range(2 * C):
                if m == C:
                    n = J_WVG
                    copy(n, row_weights[:, :, 1:1 + EM], bank[n % 8][:, 0:C * EM].rearrange("p (c e) -> p c e", c=C))
                    act.wait_ge(pre_act, copies("act", J_WVG))
                    nc.scalar.activation(row_split[:, 0, :, :], row_weights[:, :, :], ACT.Copy, scale=WSCALE)\
                        .then_inc(rows_split, 1)
                n = J_KEYS[m]
                c, h = m // 2, m % 2
                dst = keys[:, :].rearrange("p (b c k) -> p b c k", b=B, c=C)[:, 4 * h:4 * h + 4, c, 0:K]
                copy(n, dst, bank[n % 8][:, 0:4 * K].rearrange("p (b k) -> p b k", b=4), SCALE / WSCALE)
                if m % C == 0:
                    act.wait_ge(w_early[2 + m // C], 32)
                for q in range(2):
                    high(2 * NW + 2 * m + q)
            act.wait_ge(consts, NCONST)
            for h in range(2):
                n = J_KB + h
                copy(n, key_bias[:, :].rearrange("o (b k) -> o b k", b=B)[:, 4 * h:4 * h + 4, 0:K],
                     bank[n % 8][0:1 + EM, 0:4 * K].rearrange("p (b k) -> p b k", b=4), 1.0 / WSCALE)
            act.wait_ge(pre_act, copies("act", J_KB + 1))
            nc.scalar.activation(bias_split[:, 0, :], key_bias[0:1, :], ACT.Copy).then_inc(bias_parts, 1)
            for e in range(NEARLY - 2, NEARLY):
                act.wait_ge(w_early[e], 32)
                for n in range(e * NW, (e + 1) * NW):
                    high(n)

            def normalise(t, j, turn):
                act.wait_ge(x_in[j], turn * 16 + 16)
                need(act, tx_done, t)
                nc.scalar.activation(xn, xs[:, j, :], ACT.Identity, bias=nmr1[:, bass.ds(t, 1)],
                                     scale=rstd1[:, bass.ds(t, 1)]).then_inc(xn_ready, 1)

            def xT(t, j):
                act.wait_ge(tx_done, t + 1)
                need(act, s_done, t - 1)
                nc.scalar.activation(xnT[j % 2], bank[0][:, :].rearrange("p (c t) -> p c t", c=C),
                                     ACT.Copy).then_inc(xT_done, 1)

            def exp(t, j):
                act.wait_ge(s_read, 2 * t + 2)
                need(act, pt_done, t - 1)
                nc.scalar.activation(prob[j % 2], bank[2 + j % 2][:, 0:K], ACT.Exp, bias=negmax[:, j:j + 1],
                                     accum_out=rowsum[:, j:j + 1]).then_inc(exp_done, 1)

            def spread(t, j):
                act.wait_ge(x1_done, 2 * t + 2)
                need(act, stats2, t)
                nc.scalar.activation(squares[:, :], rows[:, j, 0:D], ACT.Square, bias=z[:, j, E:EM],
                                     accum_out=sum_sq[:, j:j + 1]).then_inc(stats2, 1)

            def step(k, j, turn):
                if is_tile(k):
                    xT(k, j)
                if is_tile(k - 4) and (j - 4) % G == G - 1:
                    spread(k - 4, (j - 4) % U)
                if is_tile(k + 1):
                    normalise(k + 1, (j + 1) % U, turn + (j + 1) // U)
                if is_tile(k - 1):
                    exp(k - 1, (j - 1) % U)
                if is_tile(k - 4) and (j - 4) % G < G - 1:
                    spread(k - 4, (j - 4) % U)

            act.wait_ge(scal1, 3)
            act.wait_ge(pre_mm, NJOBS)
            for k in range(-1, U - 1):
                step(k, k % U, k // U)
            act.wait_ge(w_late, 32)
            with act.Fori(1, NTURN) as i:
                for j in range(U):
                    step(i * U + j - 1, (j - 1) % U, i + (j - 1) // U)
                    if j % G == 0:
                        high(NEARLY * NW + 2 * (i - 1) + j // G)
            for n in range(NEARLY * NW + 2 * (NTURN - 1), E * NW):
                k = NT - 1 + n - (NEARLY * NW + 2 * (NTURN - 1))
                if k < NT + 4:
                    step(k, k % U, k // U)
                if n >= (E - 1) * NW:
                    act.wait_ge(w_last[n % NW], 16)
                high(n)

            nc.scalar.activation(rinv[:, 0:1], half[:, 0:1], ACT.Gelu)
            for u in range(U):
                act.wait_ge(sent[u], 16 * NTURN)

            def x2T_high(j):
                act.wait_ge(tx2_done, j + 1)
                act.wait_ge(h_done, j)
                nc.scalar.activation(x2T[:, 0, :, :], bank[0][:, :].rearrange("p (c t) -> p c t", c=C),
                                     ACT.Copy).then_inc(x2h_done, 1)

            def gelu(j):
                act.wait_ge(hb_done, j + 1)
                act.wait_ge(tg_done, j)
                nc.scalar.activation(gel, hid, ACT.Gelu).then_inc(g_done, 1)

            def gT_high(j):
                act.wait_ge(tg_done, j + 1)
                act.wait_ge(y_done, j)
                nc.scalar.activation(gelT[:, 0, :, :], bank[2][:, :].rearrange("p (c t) -> p c t", c=C),
                                     ACT.Copy).then_inc(gh_done, 1)

            x2T_high(0)
            gelu(0)
            x2T_high(1)
            gT_high(0)
            with act.Fori(1, NJ - 1) as j:
                x2T_high(j + 1)
                gelu(j)
                gT_high(j)
            gelu(NJ - 1)
            gT_high(NJ - 1)

        @block.vector
        def _(dve):
            seq = Count(dve_seq)

            def link(ins):
                seq.inc(ins)
                dve.wait_ge(dve_seq, seq.value)


            def ready(n):
                assert jobs[n] == "dve"
                dve.wait_ge(pre_mm, n + 1)

            def low_part(n, a, src, scale=1.0):
                assert jobs[n] == "both"
                dve.wait_ge(pre_act, copies("act", n))
                nc.vector.scalar_tensor_tensor(a[1], src, scale, a[0], ALU.mult, ALU.subtract).then_inc(pre_dve, 1)

            def moments_of_x(n):
                dve.wait_ge(xg_in[n % NM], 16 * (n // NM + 1))
                for u in range(M):
                    seq.inc(nc.vector.bn_stats(stats[:, u, :], xm[:, M * (n % NM) + u, :]))
                dve.wait_ge(dve_seq, seq.value)
                for u in range(M):
                    nc.vector.bn_aggr(mv1[:, M * n + u, :], stats[:, u, :]).then_inc(stats1, 1)
                dve.wait_ge(stats1, M * (n + 1))

            moments_of_x(0)
            for k in range(C):
                n = J_KQ + k
                low_part(n, [kq[:, h, k, :] for h in range(2)], bank[n % 8][:, :], WSCALE)
                if k == 1:
                    moments_of_x(1)
            n = J_BIAS
            ready(n)
            nc.vector.tensor_copy(bcol[:, :], bank[n % 8][:, 0:3 * C]).then_inc(pre_dve, 1)
            dve.wait_ge(pre_dve, copies("dve", J_BIAS))
            n = J_GSUM
            ready(n)
            dve.wait_ge(ld["wg"], 16)
            nc.vector.scalar_tensor_tensor(wg_mid[:, :, 0:E], bank[n % 8][:, 0:E].unsqueeze(1).to_broadcast([P, C, E]),
                                           -1.0 / D, wg_sb[:, :, :], ALU.mult, ALU.add).then_inc(pre_dve, 1)
            for b in range(B):
                n = J_CTX + b
                low_part(n, [ctxT[:, h, :, K * b:K * (b + 1)] for h in range(2)],
                     bank[n % 8][:, 0:C * K].rearrange("p (c s) -> p c s", c=C))

            def low(n):
                dve.wait_ge(high_done, n + 1)
                nc.vector.scalar_tensor_tensor(w_split[:, bass.ds(n * 2 * D + D, D)], wall[:, bass.ds((n + GAP) * D, D)],
                                               WSCALE, w_split[:, bass.ds(n * 2 * D, D)], ALU.mult,
                                               ALU.subtract).then_inc(low_done, 1)

            at_group = [0] * 6 + [2] * 4 + [4] * 2 + [2] * 3 + [NW + 2]
            n_low = 0
            for n in range(2, NT // M):
                moments_of_x(n)
                if n == 5:
                    dve.wait_ge(pre_mm, J_CTX + B)
                    link(nc.vector.tensor_copy(bv_bc, bcol[:, C:2 * C].unsqueeze(2).to_broadcast([P, C, P])))
                    link(nc.vector.tensor_copy(bo_cb, bcol[:, 2 * C:3 * C].unsqueeze(2).to_broadcast([P, C, P])))
                    k = 0
                    low_part(J_OV + k, [ov[:, h, k, :] for h in range(2)], bank[(J_OV + k) % 8][:, :], WSCALE)
                if 6 <= n < 6 + C - 1:
                    k = n - 5
                    low_part(J_OV + k, [ov[:, h, k, :] for h in range(2)], bank[(J_OV + k) % 8][:, :], WSCALE)
                for m in range(at_group[n]):
                    low(n_low + m)
                    if n == NT // M - 1 and m == 1:
                        dve.wait_ge(rows_split, 1)
                        nc.vector.scalar_tensor_tensor(row_split[:, 1, :, :], row_weights[:, :, :], WSCALE,
                                                       row_split[:, 0, :, :], ALU.mult, ALU.subtract)\
                            .then_inc(rows_split, 1)
                n_low += at_group[n]
            assert n_low == (NEARLY - 2) * NW
            keys4 = keys[:, :].rearrange("p (b c k) -> p b c k", b=B, c=C)
            for c in range(C):
                link(nc.vector.tensor_copy(keys4[:, :, c, K:P], wg_mid[:, c:c + 1, 0:E].to_broadcast([P, B, E])))
            n = J_VB
            ready(n)
            dve.wait_ge(ld["bo"], 16)
            nc.vector.tensor_tensor(val_bias, bank[n % 8][:, :], bo_bc, ALU.add).then_inc(pre_dve, 1)
            n = J_VGB
            ready(n)
            nc.vector.tensor_copy(vg_bias[:, :], bank[n % 8][:, 0:EM]).then_inc(pre_dve, 1)
            dve.wait_ge(pre_dve, copies("dve", J_VGB))
            n = J_VG
            ready(n)
            nc.vector.tensor_tensor(val_gate[:, :].rearrange("p (b e) -> p b e", b=B),
                                    bank[n % 8][0:K, 0:B * (1 + EM)].rearrange("p (b e) -> p b e", b=B)[:, :, 1:1 + EM],
                                    vg_bias[0:K, :].unsqueeze(1).to_broadcast([K, B, EM]), ALU.add).then_inc(pre_dve, 1)
            dve.wait_ge(bias_parts, 1)
            nc.vector.tensor_tensor(bias_split[:, 1, :], key_bias[0:1, :], bias_split[:, 0, :], ALU.subtract)\
                .then_inc(bias_parts, 1)
            dve.wait_ge(pad_out, 16 * (E + 1))
            for b in range(B):
                n = J_VAL + b
                ready(n)
                nc.vector.scalar_tensor_tensor(vals[0:K, D * b:D * (b + 1)], bank[n % 8][0:K, :], 1.0 / WSCALE,
                                               val_bias[0:K, :], ALU.mult, ALU.add).then_inc(pre_dve, 1)
                for m in range(2):
                    low((NEARLY - 2) * NW + 2 * b + m)

            dve.wait_ge(ld["bg"], 16)
            dve.wait_ge(scal1, 3)

            def pick_experts(c, n, g):
                def link(ins):
                    c.inc(ins)
                    dve.wait_ge(dve_seq, c.value)

                def over_e(a):
                    return a.unsqueeze(2).to_broadcast([P, G, E])

                def over_t(a):
                    return a.unsqueeze(1).to_broadcast([P, G, E])

                dve.wait_ge(scal2, n + 1)
                link(nc.vector.tensor_reduce(zm[:, :], zl[:, :, :], AX.X, ALU.max))
                link(nc.vector.tensor_tensor(zt[:, :, :], zl[:, :, :], over_e(zm[:, :]), ALU.is_equal))
                link(nc.vector.tensor_tensor(zt[:, :, :], zt[:, :, :], over_t(first_pick[:, :]), ALU.mult))
                link(nc.vector.tensor_reduce(zm[:, :], zt[:, :, :], AX.X, ALU.max))
                nc.vector.tensor_tensor(pick[:, :, :], over_t(first_pick[:, :]), over_e(zm[:, :]),
                                        ALU.is_equal).then_inc(picked, 1)

            def place(c, n, g):
                gs = slice(G * g, G * (g + 1))

                def link(ins):
                    c.inc(ins)
                    dve.wait_ge(dve_seq, c.value)

                dve.wait_ge(ranked, n + 1)
                link(nc.vector.tensor_tensor(zt[:, :, :], bank[1][:, 0:G * E].rearrange("p (t e) -> p t e", t=G),
                                             pick[:, :, :], ALU.mult))
                with nc.allow_low_precision(reason="row numbers and counts below 64 are exact"):
                    nc.vector.tensor_reduce(slot_i[:, gs], zt[:, :, :], AX.X, ALU.add).then_inc(slotted, 1)
                    link(nc.vector.tensor_reduce(picks[:, :], pick[:, :, :].rearrange("p t e -> p e t"), AX.X,
                                                 ALU.add))
                link(nc.vector.tensor_tensor(seen[:, 1 - g, :], seen[:, g, :], picks[:, :], ALU.add))

            def read_scores(t, j):
                dve.wait_ge(s_done, t + 1)
                nc.vector.tensor_scalar(za[:, bass.ds(t * EM, E)], bank[2 + j % 2][:, K:P], std1[:, bass.ds(t, 1)], None,
                                        ALU.mult).then_inc(s_read, 1)
                nc.vector.tensor_reduce(negmax[:, j:j + 1], bank[2 + j % 2][:, 0:K], AX.X, ALU.max,
                                        negate=True).then_inc(s_read, 1)

            def pT(t, j):
                dve.wait_ge(pt_done, t + 1)
                need(dve, pv_done, t - 1)
                nc.vector.tensor_copy(probT[j % 2], bank[4 + j % 2][0:K, 0:P]).then_inc(pT_done, 1)

            def mixed(c, t, j, turn):
                dve.wait_ge(exp_done, t + 1)
                c.inc(nc.vector.reciprocal(rinv[:, j:j + 1], rowsum[:, j:j + 1]))
                dve.wait_ge(dve_seq, c.value)
                dve.wait_ge(pv_done, t + 1)
                nc.vector.scalar_tensor_tensor(z[:, j, :], bank[4 + j % 2][:, P:P + EM], rinv[:, j:j + 1],
                                               za[:, bass.ds(t * EM, EM)], ALU.mult, ALU.add).then_inc(x1_done, 1)
                need(dve, sent[j], 16 * turn)
                nc.vector.scalar_tensor_tensor(rows[:, j, 0:D], bank[6 + j % 2][:, :], rinv[:, j:j + 1],
                                               xs[:, j, :], ALU.mult, ALU.add).then_inc(x1_done, 1)

            def step(c, k, j, turn):
                if j % G == 1 and is_tile(k - 9):
                    place(c, 2 * turn + (j - 9) // G, (j - 9) // G % 2)
                if is_tile(k - 1):
                    read_scores(k - 1, (j - 1) % U)
                if is_tile(k - 2):
                    pT(k - 2, (j - 2) % U)
                if is_tile(k - 3):
                    mixed(c, k - 3, (j - 3) % U, turn if j >= 3 else turn - 1)
                if j % G == G - 1 and is_tile(k - 7):
                    pick_experts(c, 2 * turn + (j - 7) // G, (j - 7) // G % 2)

            for k in range(U):
                step(seq, k, k, 0)
            per_turn = U + 2 * (4 + 3)
            start = seq.value
            with dve.Fori(1, NTURN) as i:
                c = Count(dve_seq, start + i * per_turn - per_turn)
                for j in range(U):
                    step(c, i * U + j, j, i)
                    if j % G == 2:
                        low(NEARLY * NW + 2 * (i - 1) + j // G)
                assert c.n == per_turn, c.n
            c = Count(dve_seq, start + (NTURN - 1) * per_turn)
            n_low = NEARLY * NW + 2 * (NTURN - 1)
            for k in range(NT, NT + U):
                step(c, k, k % U, k // U)
                for n in range((1, 1, 3, 0, 0, 0, 0, 0)[k - NT]):
                    low(n_low)
                    n_low += 1

            def link(ins):
                c.inc(ins)
                dve.wait_ge(dve_seq, c.value)

            nc.vector.engine_nop().then_inc(pairs_counted, 1)
            dve.wait_ge(counted, 1)
            end_row = bank[1][:, 0:E]
            link(nc.vector.scalar_tensor_tensor(ti[:, :], end_row, float(P - 1), base_row[:, :], ALU.add, ALU.subtract))
            link(nc.vector.tensor_single_scalar(ti[:, :], ti[:, :], P.bit_length() - 1, ALU.arith_shift_right))
            link(nc.vector.tensor_copy(cum[:, 0, 4:], ti[:, :]))
            for s, sh in enumerate((1, 2, 4)):
                link(nc.vector.tensor_tensor(cum[:, s + 1, 4:], cum[:, s, 4:], cum[:, s, 4 - sh:4 - sh + E], ALU.add))
            link(nc.vector.tensor_tensor(vrow[:, :], cum[:, 3, 4:], cum[:, 0, 4:], ALU.subtract))
            link(nc.vector.scalar_tensor_tensor(vrow[:, :], vrow[:, :], float(P), end_row, ALU.mult, ALU.add))
            shape = [P, NJ, E]
            link(nc.vector.tensor_tensor(ge[:, :, :], jota[:, :].unsqueeze(2).to_broadcast(shape),
                                         cum[:, 3:4, 4:].to_broadcast(shape), ALU.is_ge))
            link(nc.vector.tensor_reduce(tv[:, 0, :], ge[:, :, :], AX.X, ALU.add))
            link(nc.vector.tensor_tensor(ge[:, :, :], tv[:, 0, :].unsqueeze(2).to_broadcast(shape),
                                         eota[:, :].unsqueeze(1).to_broadcast(shape), ALU.is_equal))
            link(nc.vector.tensor_reduce(tv[:, 1, :], ge[:, :, :], AX.X, ALU.add))
            link(nc.vector.tensor_tensor(ge[:, :, :], ge[:, :, :], vrow[:, :].unsqueeze(1).to_broadcast(shape), ALU.mult))
            link(nc.vector.tensor_reduce(tv[:, 2, :], ge[:, :, :], AX.X, ALU.add))
            link(nc.vector.tensor_tensor(tv[:, 1, :], negj[:, :], tv[:, 1, :], ALU.mult))
            nc.vector.scalar_tensor_tensor(table[:, 0, :], tv[:, 1, :], float(DUMMY), tv[:, 2, :], ALU.add,
                                           ALU.add).then_inc(tabled, 1)
            for n, width in ((1, NW * 2 * D), (2, D)):
                nc.vector.tensor_scalar(table[:, n, :], tv[:, 0, :], float(E - 1), float(width), ALU.min,
                                        ALU.mult).then_inc(tabled, 1)
            dve.wait_ge(tabled, 3)
            for n in range(n_low, E * NW):
                low(n)

            dve.wait_ge(b1_in, 16)
            for u in range(U):
                dve.wait_ge(sent[u], 16 * NTURN)

            def bias(j):
                ex = dve.value_load(table[0:1, 2, bass.ds(j, 1)], min_val=0, max_val=(E - 1) * D)
                dve.wait_ge(h_done, j + 1)
                dve.wait_ge(g_done, j)
                nc.vector.scalar_tensor_tensor(hid, bank[1][:, :], 1.0 / WSCALE, keys[:, bass.ds(ex, D)], ALU.mult,
                                               ALU.add).then_inc(hb_done, 1)

            def x2T_low(j):
                dve.wait_ge(x2h_done, j + 1)
                nc.vector.tensor_tensor(x2T[:, 1, :, :], bank[0][:, :].rearrange("p (c t) -> p c t", c=C),
                                        x2T[:, 0, :, :], ALU.subtract).then_inc(x2l_done, 1)

            def gT_low(j):
                dve.wait_ge(gh_done, j + 1)
                nc.vector.tensor_tensor(gelT[:, 1, :, :], bank[2][:, :].rearrange("p (c t) -> p c t", c=C),
                                        gelT[:, 0, :, :], ALU.subtract).then_inc(gl_done, 1)

            def finish(j, r):
                dve.wait_ge(y_done, j + 1)
                dve.wait_ge(res_ready, j + 1 + R)
                nc.vector.scalar_tensor_tensor(res[r], bank[3][:, :], 1.0 / WSCALE, res[r], ALU.mult,
                                               ALU.add).then_inc(out_done, 1)

            def step(j, r):
                if not isinstance(j, int) or j + 1 < NJ:
                    bias(j + 1)
                if not isinstance(j, int) or j + 2 < NJ:
                    x2T_low(j + 2)
                finish(j, r)
                if not isinstance(j, int) or j + 1 < NJ:
                    gT_low(j + 1)

            x2T_low(0)
            bias(0)
            x2T_low(1)
            gT_low(0)
            with dve.Fori(0, NJTURN - 1) as i:
                for r in range(R):
                    step(i * R + r, r)
            for r in range(R):
                step(NJ - R + r, r)

        @block.tensor
        def _(pe):
            mm = nc.tensor.matmul
            PARTS = ((0, 0), (0, 1), (1, 0))

            def free(n):
                if n >= 8:
                    copied(pe, n - 8)

            for e in range(C):
                pe.wait_ge(wkq_in[e], 32)
                for k in range(C):
                    last = mm(bank[(J_KQ + k) % 8][:, :], wk_sb[:, e, P * k:P * (k + 1)], wq_sb[:, e, :],
                              start=(e == 0), stop=(e == C - 1))
                    if e == C - 1:
                        last.then_inc(pre_mm, 1)
            pe.wait_ge(consts, NCONST)
            pe.wait_ge(ld["bias"], 48)
            n = J_BIAS
            nc.tensor.transpose(bank[n % 8][:, 0:3 * C], brow12[:, :], ident[0:3 * C, 0:3 * C]).then_inc(pre_mm, 1)
            pe.wait_ge(ld["wg"], 16)
            n = J_GSUM
            for e in range(C):
                last = mm(bank[n % 8][:, 0:E], ones_f[:, :], wg_sb[:, e, :], start=(e == 0), stop=(e == C - 1))
            last.then_inc(pre_mm, 1)
            pe.wait_ge(ld["ctx"], 16)
            for b in range(B):
                n = J_CTX + b
                free(n)
                for c in range(C):
                    last = nc.tensor.transpose(bank[n % 8][:, K * c:K * (c + 1)], ctx_nat[0:K, b, P * c:P * (c + 1)],
                                               ident[0:K, 0:K])
                last.then_inc(pre_mm, 1)
            pe.wait_ge(ld["wo"], 16)
            for k in range(C):
                n = J_WOT + k
                free(n)
                for c in range(C):
                    last = nc.tensor.transpose(bank[n % 8][:, P * c:P * (c + 1)], wo_sb[:, c, P * k:P * (k + 1)],
                                               ident[:, :])
                last.then_inc(pre_mm, 1)
            def small(n, i, w, cols, width):
                k, e = i // C, i % C
                return mm(bank[n % 8][:, width * k:width * (k + 1)], w[:, e, P * k:P * (k + 1)], cols[e],
                          start=(e == 0), stop=(e == C - 1))

            pe.wait_ge(ld["wv"], 16)
            for k in range(C):
                copied(pe, J_WOT + k)
            copied(pe, J_BIAS)
            copied(pe, J_GSUM)
            free(J_U)
            free(J_WOG)
            bq_cols = [bcol[:, e:e + 1] for e in range(C)]
            wg_cols = [wg_mid[:, e, :] for e in range(C)]
            for k in range(C):
                n = J_OV + k
                free(n)
                for e in range(C):
                    last = mm(bank[n % 8][:, :], wv_sb[:, e, P * k:P * (k + 1)], woT[:, e, :],
                              start=(e == 0), stop=(e == C - 1))
                    last_u = small(J_U, C * k + e, wk_sb, bq_cols, 1)
                    last_wog = small(J_WOG, C * k + e, wo_sb, wg_cols, EM)
                last.then_inc(pre_mm, 1)
            last_u.then_inc(pre_mm, 1)
            last_wog.then_inc(pre_mm, 1)
            for k in range(C):
                copied(pe, J_KQ + k)
            for b in range(B):
                copied(pe, J_CTX + b)
            copied(pe, J_WOG)
            free(J_WVG)
            wo_cols = [wo_gate[:, e, :] for e in range(C)]
            for c in range(C):
                for h in range(2):
                    n = J_KEYS[2 * c + h]
                    free(n)
                    for k in range(C):
                        for u, v in PARTS:
                            last = mm(bank[n % 8][:, 0:4 * K], kq[:, u, k, P * c:P * (c + 1)],
                                      ctxT[:, v, k, 4 * K * h:4 * K * (h + 1)],
                                      start=(k == 0 and u + v == 0), stop=(k == C - 1 and u == 1))
                        if c < C // 2:
                            last_wvg = small(J_WVG, C * (2 * c + h) + k, wv_sb, wo_cols, EM)
                    last.then_inc(pre_mm, 1)
                    if 2 * c + h == C - 1:
                        last_wvg.then_inc(pre_mm, 1)
            n = J_VB
            free(n)
            pe.wait_ge(dve_seq, 6 * M + 2)
            for e in range(C):
                last = mm(bank[n % 8][:, :], bv_bc[:, e, :], woT[:, e, :], start=(e == 0), stop=(e == C - 1))
            last.then_inc(pre_mm, 1)
            n = J_VGB
            free(n)
            for e in range(C):
                mm(bank[n % 8][:, 0:EM], bv_bc[:, e, :], wo_gate[:, e, :], start=(e == 0), stop=False)
            for e in range(C):
                last = mm(bank[n % 8][:, 0:EM], bo_cb[:, e, :], wg_mid[:, e, :], start=False, stop=(e == C - 1))
            last.then_inc(pre_mm, 1)
            pe.wait_ge(rows_split, 2)
            for h in range(2):
                n = J_KB + h
                free(n)
                for k in range(C):
                    for u, v in PARTS:
                        last = mm(bank[n % 8][0:1 + EM, 0:4 * K], row_split[:, u, k, :],
                                  ctxT[:, v, k, 4 * K * h:4 * K * (h + 1)],
                                  start=(k == 0 and u + v == 0), stop=(k == C - 1 and u == 1))
                last.then_inc(pre_mm, 1)
            n = J_VG
            free(n)
            for h in range(2):
                copied(pe, J_KB + h)
            for b in range(B):
                last = nc.tensor.transpose(bank[n % 8][0:K, (1 + EM) * b:(1 + EM) * (b + 1)], key_bias[:, P * b:P * b + K],
                                           ident[0:1 + EM, 0:1 + EM])
            last.then_inc(pre_mm, 1)
            for k in range(C):
                copied(pe, J_OV + k)
            for b in range(B):
                n = J_VAL + b
                free(n)
                for k in range(C):
                    for u, v in PARTS:
                        last = mm(bank[n % 8][0:K, :], ctxT[:, u, k, K * b:K * (b + 1)], ov[:, v, k, :],
                                  start=(k == 0 and u + v == 0), stop=(k == C - 1 and u == 1))
                last.then_inc(pre_mm, 1)
            pe.wait_ge(pre_act, copies("act"))
            pe.wait_ge(pre_dve, copies("dve"))
            pe.wait_ge(bias_parts, 2)

            def transpose_x(t, j):
                pe.wait_ge(xn_ready, t + 1)
                need(pe, xT_done, t)
                for c in range(C):
                    last = nc.tensor.transpose(bank[0][:, P * c:P * (c + 1)], xn[:, P * c:P * (c + 1)], ident[:, :])
                last.then_inc(tx_done, 1)

            def scores(t, j, b):
                pe.wait_ge(xT_done, t + 1)
                for c in range(C):
                    mm(bank[2 + j % 2][:, 0:P], xnT[j % 2][:, c, :], keys[:, bass.ds((b * C + c) * P, P)],
                       start=(c == 0), stop=False)
                for h in range(2):
                    last = mm(bank[2 + j % 2][:, 0:P], ones_h[0:1, :], bias_split[:, h, bass.ds(b * P, P)],
                              start=False, stop=(h == 1))
                last.then_inc(s_done, 1)

            def transpose_p(t, j):
                pe.wait_ge(exp_done, t + 1)
                need(pe, x1_done, 2 * t - 3)
                nc.tensor.transpose(bank[4 + j % 2][0:K, 0:P], prob[j % 2], ident[:, :]).then_inc(pt_done, 1)

            def mix(t, j, b):
                pe.wait_ge(pT_done, t + 1)
                need(pe, x1_done, 2 * t - 2)
                mm(bank[4 + j % 2][:, P:P + EM], probT[j % 2], val_gate[:, bass.ds(b * EM, EM)], start=True, stop=True)
                mm(bank[6 + j % 2][:, :], probT[j % 2], vals[0:K, bass.ds(b * D, D)], start=True, stop=True)\
                    .then_inc(pv_done, 1)

            def rank(n, g):
                pe.wait_ge(picked, n + 1)
                o = bank[1][:, 0:G * E]
                mm(o, before[:, :], pick[:, :, :].rearrange("p t e -> p (t e)"), start=True, stop=False)
                for q in range(G - 1):
                    mm(bank[1][:, E * (q + 1):E * G], ones_h[:, :], pick[:, q:q + 1, :].to_broadcast([P, G - 1 - q, E]),
                       start=False, stop=False)
                mm(o, ones_h[:, :], seen[:, g:g + 1, :].to_broadcast([P, G, E]), start=False, stop=True)\
                    .then_inc(ranked, 1)

            def step(k, j, turn):
                if is_tile(k):
                    transpose_x(k, j)
                if is_tile(k - 1):
                    scores(k - 1, (j - 1) % U, 2 * turn + (j - 1) // G)
                if is_tile(k - 2):
                    transpose_p(k - 2, (j - 2) % U)
                if is_tile(k - 3):
                    mix(k - 3, (j - 3) % U, 2 * turn + (j - 3) // G)
                if j % G == 0 and is_tile(k - 8):
                    rank(2 * turn + (j - 8) // G, (j - 8) // G % 2)

            for k in range(U):
                step(k, k, 0)
            with pe.Fori(1, NTURN) as i:
                for j in range(U):
                    step(i * U + j, j, i)
            for k in range(NT, NT + U):
                step(k, k % U, k // U)

            pe.wait_ge(pairs_counted, 1)
            mm(bank[1][:, 0:E], ones_h[:, :], seen[:, 0, :], start=True, stop=True).then_inc(counted, 1)

            pe.wait_ge(tabled, 3)
            pe.wait_ge(low_done, E * NW)

            def transpose_x2(j):
                pe.wait_ge(xn2_ready, j + 1)
                pe.wait_ge(x2l_done, j)
                for c in range(C):
                    last = nc.tensor.transpose(bank[0][:, P * c:P * (c + 1)], xn2[:, P * c:P * (c + 1)], ident[:, :])
                last.then_inc(tx2_done, 1)

            def product(o, a, first, low_ready, j):
                for c in range(C):
                    for h in range(2):
                        mm(o, a[:, 0, c, :], w_split[:, bass.ds(first + (2 * c + h) * D, D)],
                           start=(c == 0 and h == 0), stop=False)
                pe.wait_ge(low_ready, j + 1)
                for c in range(C):
                    last = mm(o, a[:, 1, c, :], w_split[:, bass.ds(first + 2 * c * D, D)], start=False, stop=(c == C - 1))
                return last

            def up(j, ex):
                pe.wait_ge(x2h_done, j + 1)
                pe.wait_ge(hb_done, j)
                product(bank[1][:, :], x2T, ex, x2l_done, j).then_inc(h_done, 1)

            def transpose_g(j):
                pe.wait_ge(g_done, j + 1)
                pe.wait_ge(gl_done, j)
                for c in range(C):
                    last = nc.tensor.transpose(bank[2][:, P * c:P * (c + 1)], gel[:, P * c:P * (c + 1)], ident[:, :])
                last.then_inc(tg_done, 1)

            def down(j, ex):
                pe.wait_ge(gh_done, j + 1)
                pe.wait_ge(out_done, j)
                product(bank[3][:, :], gelT, ex + C * 2 * D, gl_done, j).then_inc(y_done, 1)

            def experts(j, n):
                return nc.values_load_multi_w_load_instructions(
                    table[0:1, 1, bass.ds(j, n)], engines=[mybir.EngineType.PE], min_val=0,
                    max_val=(E - 1) * NW * 2 * D,
                    skip_runtime_bounds_check_because="the table is made from expert numbers held to E - 1")[1]

            transpose_x2(0)
            up(0, experts(0, 1)[0])
            transpose_x2(1)
            transpose_g(0)
            def step(j, ex, ex_before):
                up(j, ex)
                transpose_x2(j + 1)
                down(j - 1, ex_before)
                transpose_g(j)

            assert (NJ - 3) % (2 * R) == 0
            with pe.Fori(0, (NJ - 3) // (2 * R)) as i:
                ex = experts(i * 2 * R, 2 * R + 1)
                for r in range(1, 2 * R + 1):
                    step(i * 2 * R + r, ex[r], ex[r - 1])
            ex = experts(NJ - 3, 3)
            step(NJ - 2, ex[1], ex[0])
            up(NJ - 1, ex[2])
            down(NJ - 2, ex[1])
            transpose_g(NJ - 1)
            down(NJ - 1, ex[2])


_INS = ["x", "ctx_1024", "L0_xattn_Wk", "L0_xattn_Wv", "L0_xattn_bv", "L0_xattn_Wq", "L0_xattn_bq", "L0_xattn_Wo",
        "L0_xattn_bo", "L0_ffn_Wg", "L0_ffn_bg", "L0_ffn_W1", "L0_ffn_b1", "L0_ffn_W2", "L0_ffn_b2"]


def kernel(**inputs):
    import numpy as np
    import concourse.bacc as bacc
    from concourse.bass_utils import run_bass_kernel_spmd

    nc = bacc.Bacc("TRN2", target_bir_lowering=False, num_devices=1)
    arrays, args = {}, []
    for name in _INS:
        a = np.ascontiguousarray(inputs[name])
        arrays[f"in_{name}"] = a
        args.append(nc.dram_tensor(f"in_{name}", a.shape, mybir.dt.from_np(a.dtype), kind="ExternalInput").ap())
    args.append(nc.dram_tensor("out_x", (B, S, D), F32, kind="ExternalOutput").ap())
    build(nc, *args)
    r = run_bass_kernel_spmd(nc, [arrays], core_ids=[0])
    return r.results[0]["out_x"]
```
